# Optimizing a Trainium2 kernel written in Bass

```python
import numpy as np
import jax
import jax.numpy as jnp

def _softmax(x, axis=-1):
    return jax.nn.softmax(x, axis=axis)

def _gelu(x):
    return jax.nn.gelu(x, approximate=True)

def _silu(x):
    return jax.nn.silu(x)

def _sigmoid(x):
    return jax.nn.sigmoid(x)

def _layernorm(x, axis=-1, eps=1e-05):
    m = jnp.mean(x, axis=axis, keepdims=True)
    v = jnp.var(x, axis=axis, keepdims=True)
    return (x - m) / jnp.sqrt(v + eps)

def _scatter_add(tgt, idx, src, axis=0):
    return tgt.at[idx].add(src)

def _segment_sum(src, seg, n):
    return jax.ops.segment_sum(src, seg, n)
kernel_name = 'mk_decoder_postln_d1_seqx_r8_2cd312'

def setup_inputs(seed: int=0):
    np.random.seed(seed)
    _w = jnp.asarray

    def _rec_inputs():
        import jax
        import jax.numpy as jnp
        _rk = jax.random.key(seed)
        x = 7.22e-05 + 1 * jax.random.normal(jax.random.fold_in(_rk, 1), (16, 256, 128), jnp.float32)
        _lenS = 256 - jax.random.randint(jax.random.fold_in(_rk, 7), (16,), 0, max(1, 256 // 4) + 1, jnp.int32)
        _lenS2 = 64 - jax.random.randint(jax.random.fold_in(_rk, 8), (16,), 0, max(1, 64 // 4) + 1, jnp.int32)
        _ctx_768P = jax.random.normal(jax.random.fold_in(_rk, 11), (16, 16, 96), jnp.float32)
        _ctx_768c = jax.random.dirichlet(jax.random.fold_in(_rk, 511), 0.3 * jnp.ones((16,), jnp.float32), (16, 64))
        _ctx_768t = jnp.einsum('bsk,bkd->bsd', _ctx_768c, _ctx_768P)
        _ctx_768t = _ctx_768t * jax.lax.rsqrt(jnp.mean(jnp.square(_ctx_768t)) + 1e-12) * 0.953939
        ctx_768 = 2.09791e-05 + 1.00001 * (_ctx_768t + 0.3 * jax.random.normal(jax.random.fold_in(_rk, 611), (16, 64, 96), jnp.float32))
        _validS = jnp.arange(256)[None, :] < _lenS[:, None]
        _validS2 = jnp.arange(64)[None, :] < _lenS2[:, None]
        _causal = jnp.tril(jnp.ones((256, 256), dtype=bool))
        mask_BxS_bk0 = jnp.logical_not(jnp.broadcast_to(_validS[:, :], (16, 256)))
        return (x, ctx_768, mask_BxS_bk0)
    x, ctx_768, mask_BxS_bk0 = _rec_inputs()

    def _L0_attn_setup():
        import jax, jax.numpy as jnp
        import numpy as np
        NUM_HEADS = 16
        NUM_UNITS = 128
        NEG = -2.0 ** 32 + 1.0
        EPS = 1e-08

        def _attention(x, Wq, bq, Wk, bk, Wv, bv, gamma, beta):
            B, T, C = x.shape
            H = NUM_HEADS
            U = NUM_UNITS
            dh = U // H
            Q = jax.nn.relu(x @ Wq + bq)
            K = jax.nn.relu(x @ Wk + bk)
            V = jax.nn.relu(x @ Wv + bv)
            Qh = Q.reshape(B, T, H, dh)
            Kh = K.reshape(B, T, H, dh)
            Vh = V.reshape(B, T, H, dh)
            scores = jnp.einsum('bqhd,bkhd->bhqk', Qh, Kh) / np.sqrt(dh)
            key_mask = jnp.sign(jnp.abs(jnp.sum(x, axis=-1)))
            scores = jnp.where(key_mask[:, None, None, :] == 0, NEG, scores)
            tril = jnp.tril(jnp.ones((T, T), dtype=scores.dtype))
            scores = jnp.where(tril[None, None, :, :] == 0, NEG, scores)
            attn = jax.nn.softmax(scores, axis=-1)
            query_mask = jnp.sign(jnp.abs(jnp.sum(x, axis=-1)))
            attn = attn * query_mask[:, None, :, None]
            out = jnp.einsum('bhqk,bkhd->bqhd', attn, Vh).reshape(B, T, U)
            out = out + x
            mean = jnp.mean(out, axis=-1, keepdims=True)
            var = jnp.mean((out - mean) ** 2, axis=-1, keepdims=True)
            normalized = (out - mean) / jnp.sqrt(var + EPS)
            return gamma * normalized + beta
        key = jax.random.key(seed)
        ks = jax.random.split(key, 8)
        B, T, C = (2, 256, 128)
        U = NUM_UNITS
        x = jax.random.normal(ks[0], (B, T, C), dtype=jnp.float32)
        s = 1.0 / np.sqrt(C)
        Wq = jax.random.normal(ks[1], (C, U), dtype=jnp.float32) * s
        Wk = jax.random.normal(ks[2], (C, U), dtype=jnp.float32) * s
        Wv = jax.random.normal(ks[3], (C, U), dtype=jnp.float32) * s
        bq = jnp.zeros((U,), dtype=jnp.float32)
        bk = jnp.zeros((U,), dtype=jnp.float32)
        bv = jnp.zeros((U,), dtype=jnp.float32)
        gamma = jnp.ones((U,), dtype=jnp.float32)
        beta = jnp.zeros((U,), dtype=jnp.float32)
        return {'x': x, 'Wq': Wq, 'bq': bq, 'Wk': Wk, 'bk': bk, 'Wv': Wv, 'bv': bv, 'gamma': gamma, 'beta': beta}
    _L0_attn_all = _L0_attn_setup()
    _L0_attn_in = {k: v for k, v in _L0_attn_all.items() if k in ('Wq', 'bq', 'Wk', 'bk', 'Wv', 'bv', 'gamma', 'beta')}
    del _L0_attn_all

    def _L0_xattn_setup():
        import jax, jax.numpy as jnp
        import numpy as np
        NUM_HEADS = 16
        key = jax.random.key(seed)
        k1, k2, k3, k4, k5 = jax.random.split(key, 5)
        B, N, C = (4, 256, 128)
        N2, Cy = (128, 96)
        x = jax.random.normal(k1, (B, N, C), dtype=jnp.float32)
        y = jax.random.normal(k2, (B, N2, Cy), dtype=jnp.float32)
        pad_mask = jax.random.randint(k3, (B, N), 0, 2).astype(jnp.bool_)
        Wq = jax.random.normal(k4, (C, C), dtype=jnp.float32) * C ** (-0.5)
        Wkv = jax.random.normal(k5, (2 * C, Cy), dtype=jnp.float32) * Cy ** (-0.5)
        return {'x': x, 'y': y, 'pad_mask': pad_mask, 'Wq': Wq, 'Wkv': Wkv}
    _L0_xattn_all = _L0_xattn_setup()
    _L0_xattn_in = {k: v for k, v in _L0_xattn_all.items() if k in ('Wq', 'Wkv')}
    del _L0_xattn_all

    def _L0_ffn_setup():
        import jax, jax.numpy as jnp
        import numpy as np
        B, S, D, H, L, E, K = (4, 128, 128, 16, 2, 8, 2)
        DFF = 4 * D

        def _ln(x, w, b):
            m = x.mean(-1, keepdims=True)
            v = x.var(-1, keepdims=True)
            return (x - m) / jnp.sqrt(v + 1e-05) * w + b

        def _attn(x, wq, wk, wv, wo, bq, bk, bv, bo):
            Bb, T, C = x.shape
            hd = C // H
            q = (x @ wq + bq).reshape(Bb, T, H, hd).transpose(0, 2, 1, 3)
            k = (x @ wk + bk).reshape(Bb, T, H, hd).transpose(0, 2, 1, 3)
            v = (x @ wv + bv).reshape(Bb, T, H, hd).transpose(0, 2, 1, 3)
            att = jnp.einsum('bhqd,bhkd->bhqk', q, k) * hd ** (-0.5)
            causal = jnp.tril(jnp.ones((T, T), bool))
            att = jnp.where(causal, att, -jnp.inf)
            att = jax.nn.softmax(att, axis=-1)
            y = jnp.einsum('bhqk,bhkd->bhqd', att, v).transpose(0, 2, 1, 3).reshape(Bb, T, C)
            return y @ wo + bo

        def _ffn(h, w1, b1, w2, b2):
            return jax.nn.gelu(h @ w1 + b1, approximate=False) @ w2 + b2

        def _combine_weights(logits):
            vals, idx = jax.lax.top_k(logits, K)
            w = jax.nn.softmax(vals, axis=-1)
            onehot = (idx[..., None] == jnp.arange(E)).astype(w.dtype)
            return jnp.sum(w[..., None] * onehot, axis=-2)

        def _token_moe(h, gw, gb, w1, b1, w2, b2):
            cw = _combine_weights(h @ gw + gb)
            out = jnp.zeros_like(h)
            for e in range(E):
                out = out + _ffn(h, w1[e], b1[e], w2[e], b2[e]) * cw[..., e:e + 1]
            return out

        def _seq_moe(h, gw, gb, w1, b1, w2, b2):
            cw = _combine_weights(h.mean(axis=1) @ gw + gb)
            out = jnp.zeros_like(h)
            for e in range(E):
                out = out + _ffn(h, w1[e], b1[e], w2[e], b2[e]) * cw[:, e, None, None]
            return out
        key = jax.random.key(seed)
        ks = jax.random.split(key, 9)
        n = lambda k, shp: jax.random.normal(k, shp, dtype=jnp.float32) * 0.02
        return {'x': jax.random.normal(ks[0], (B, S, D), dtype=jnp.float32), 'ln1_w': jnp.ones((L, D), jnp.float32), 'ln1_b': jnp.zeros((L, D), jnp.float32), 'ln2_w': jnp.ones((L, D), jnp.float32), 'ln2_b': jnp.zeros((L, D), jnp.float32), 'wq': n(ks[1], (L, D, D)), 'wk': n(ks[2], (L, D, D)), 'wv': n(ks[3], (L, D, D)), 'wo': n(ks[4], (L, D, D)), 'bq': jnp.zeros((L, D), jnp.float32), 'bk': jnp.zeros((L, D), jnp.float32), 'bv': jnp.zeros((L, D), jnp.float32), 'bo': jnp.zeros((L, D), jnp.float32), 'gate_w': n(ks[5], (L, D, E)), 'gate_b': jnp.zeros((L, E), jnp.float32), 'e_w1': n(ks[6], (L, E, D, DFF)), 'e_b1': jnp.zeros((L, E, DFF), jnp.float32), 'e_w2': n(ks[7], (L, E, DFF, D)), 'e_b2': jnp.zeros((L, E, D), jnp.float32)}
    _L0_ffn_all = _L0_ffn_setup()
    _L0_ffn_in = {k: v for k, v in _L0_ffn_all.items() if k in ('ln1_w', 'ln1_b', 'ln2_w', 'ln2_b', 'wq', 'wk', 'wv', 'wo', 'bq', 'bk', 'bv', 'bo', 'gate_w', 'gate_b', 'e_w1', 'e_b1', 'e_w2', 'e_b2')}
    del _L0_ffn_all
    return {'x': x, 'ctx_768': ctx_768, 'mask_BxS_bk0': mask_BxS_bk0, 'L0_attn_Wq': _L0_attn_in['Wq'], 'L0_attn_bq': _L0_attn_in['bq'], 'L0_attn_Wk': _L0_attn_in['Wk'], 'L0_attn_bk': _L0_attn_in['bk'], 'L0_attn_Wv': _L0_attn_in['Wv'], 'L0_attn_bv': _L0_attn_in['bv'], 'L0_attn_gamma': _L0_attn_in['gamma'], 'L0_attn_beta': _L0_attn_in['beta'], 'L0_xattn_Wq': _L0_xattn_in['Wq'], 'L0_xattn_Wkv': _L0_xattn_in['Wkv'], 'L0_ffn_ln1_w': _L0_ffn_in['ln1_w'], 'L0_ffn_ln1_b': _L0_ffn_in['ln1_b'], 'L0_ffn_ln2_w': _L0_ffn_in['ln2_w'], 'L0_ffn_ln2_b': _L0_ffn_in['ln2_b'], 'L0_ffn_wq': _L0_ffn_in['wq'], 'L0_ffn_wk': _L0_ffn_in['wk'], 'L0_ffn_wv': _L0_ffn_in['wv'], 'L0_ffn_wo': _L0_ffn_in['wo'], 'L0_ffn_bq': _L0_ffn_in['bq'], 'L0_ffn_bk': _L0_ffn_in['bk'], 'L0_ffn_bv': _L0_ffn_in['bv'], 'L0_ffn_bo': _L0_ffn_in['bo'], 'L0_ffn_gate_w': _L0_ffn_in['gate_w'], 'L0_ffn_gate_b': _L0_ffn_in['gate_b'], 'L0_ffn_e_w1': _L0_ffn_in['e_w1'], 'L0_ffn_e_b1': _L0_ffn_in['e_b1'], 'L0_ffn_e_w2': _L0_ffn_in['e_w2'], 'L0_ffn_e_b2': _L0_ffn_in['e_b2']}

def reference(x, ctx_768, mask_BxS_bk0, L0_attn_Wq, L0_attn_bq, L0_attn_Wk, L0_attn_bk, L0_attn_Wv, L0_attn_bv, L0_attn_gamma, L0_attn_beta, L0_xattn_Wq, L0_xattn_Wkv, L0_ffn_ln1_w, L0_ffn_ln1_b, L0_ffn_ln2_w, L0_ffn_ln2_b, L0_ffn_wq, L0_ffn_wk, L0_ffn_wv, L0_ffn_wo, L0_ffn_bq, L0_ffn_bk, L0_ffn_bv, L0_ffn_bo, L0_ffn_gate_w, L0_ffn_gate_b, L0_ffn_e_w1, L0_ffn_e_b1, L0_ffn_e_w2, L0_ffn_e_b2):
    import jax
    import jax.numpy as jnp

    def _L0_attn_ref(x, Wq, bq, Wk, bk, Wv, bv, gamma, beta):
        import jax, jax.numpy as jnp
        import numpy as np
        NUM_HEADS = 16
        NUM_UNITS = 128
        NEG = -2.0 ** 32 + 1.0
        EPS = 1e-08

        def _attention(x, Wq, bq, Wk, bk, Wv, bv, gamma, beta):
            B, T, C = x.shape
            H = NUM_HEADS
            U = NUM_UNITS
            dh = U // H
            Q = jax.nn.relu(x @ Wq + bq)
            K = jax.nn.relu(x @ Wk + bk)
            V = jax.nn.relu(x @ Wv + bv)
            Qh = Q.reshape(B, T, H, dh)
            Kh = K.reshape(B, T, H, dh)
            Vh = V.reshape(B, T, H, dh)
            scores = jnp.einsum('bqhd,bkhd->bhqk', Qh, Kh) / np.sqrt(dh)
            key_mask = jnp.sign(jnp.abs(jnp.sum(x, axis=-1)))
            scores = jnp.where(key_mask[:, None, None, :] == 0, NEG, scores)
            tril = jnp.tril(jnp.ones((T, T), dtype=scores.dtype))
            scores = jnp.where(tril[None, None, :, :] == 0, NEG, scores)
            attn = jax.nn.softmax(scores, axis=-1)
            query_mask = jnp.sign(jnp.abs(jnp.sum(x, axis=-1)))
            attn = attn * query_mask[:, None, :, None]
            out = jnp.einsum('bhqk,bkhd->bqhd', attn, Vh).reshape(B, T, U)
            out = out + x
            mean = jnp.mean(out, axis=-1, keepdims=True)
            var = jnp.mean((out - mean) ** 2, axis=-1, keepdims=True)
            normalized = (out - mean) / jnp.sqrt(var + EPS)
            return gamma * normalized + beta
        return _attention(x, Wq, bq, Wk, bk, Wv, bv, gamma, beta)

    def _L0_xattn_ref(x, y, pad_mask, Wq, Wkv):
        import jax, jax.numpy as jnp
        import numpy as np
        NUM_HEADS = 16
        B, N, C = x.shape
        N2 = y.shape[1]
        H = NUM_HEADS
        d = C // H
        scale = d ** (-0.5)
        q = (x @ Wq.T).reshape(B, N, H, d).transpose(0, 2, 1, 3)
        kv = (y @ Wkv.T).reshape(B, N2, 2, H, d).transpose(2, 0, 3, 1, 4)
        k, v = (kv[0], kv[1])
        attn = jnp.einsum('bhnd,bhmd->bhnm', q * scale, k)
        attn = jnp.where(pad_mask[:, None, :, None], attn, jnp.float32(-1000000000.0))
        attn = jax.nn.softmax(attn, axis=-1)
        out = jnp.einsum('bhnm,bhmd->bhnd', attn, v)
        return out.transpose(0, 2, 1, 3).reshape(B, N, C)

    def _L0_ffn_ref(x, ln1_w, ln1_b, ln2_w, ln2_b, wq, wk, wv, wo, bq, bk, bv, bo, gate_w, gate_b, e_w1, e_b1, e_w2, e_b2):
        import jax, jax.numpy as jnp
        import numpy as np
        B, S, D, H, L, E, K = (4, 128, 128, 16, 2, 8, 2)
        DFF = 4 * D

        def _ln(x, w, b):
            m = x.mean(-1, keepdims=True)
            v = x.var(-1, keepdims=True)
            return (x - m) / jnp.sqrt(v + 1e-05) * w + b

        def _attn(x, wq, wk, wv, wo, bq, bk, bv, bo):
            Bb, T, C = x.shape
            hd = C // H
            q = (x @ wq + bq).reshape(Bb, T, H, hd).transpose(0, 2, 1, 3)
            k = (x @ wk + bk).reshape(Bb, T, H, hd).transpose(0, 2, 1, 3)
            v = (x @ wv + bv).reshape(Bb, T, H, hd).transpose(0, 2, 1, 3)
            att = jnp.einsum('bhqd,bhkd->bhqk', q, k) * hd ** (-0.5)
            causal = jnp.tril(jnp.ones((T, T), bool))
            att = jnp.where(causal, att, -jnp.inf)
            att = jax.nn.softmax(att, axis=-1)
            y = jnp.einsum('bhqk,bhkd->bhqd', att, v).transpose(0, 2, 1, 3).reshape(Bb, T, C)
            return y @ wo + bo

        def _ffn(h, w1, b1, w2, b2):
            return jax.nn.gelu(h @ w1 + b1, approximate=False) @ w2 + b2

        def _combine_weights(logits):
            vals, idx = jax.lax.top_k(logits, K)
            w = jax.nn.softmax(vals, axis=-1)
            onehot = (idx[..., None] == jnp.arange(E)).astype(w.dtype)
            return jnp.sum(w[..., None] * onehot, axis=-2)

        def _token_moe(h, gw, gb, w1, b1, w2, b2):
            cw = _combine_weights(h @ gw + gb)
            out = jnp.zeros_like(h)
            for e in range(E):
                out = out + _ffn(h, w1[e], b1[e], w2[e], b2[e]) * cw[..., e:e + 1]
            return out

        def _seq_moe(h, gw, gb, w1, b1, w2, b2):
            cw = _combine_weights(h.mean(axis=1) @ gw + gb)
            out = jnp.zeros_like(h)
            for e in range(E):
                out = out + _ffn(h, w1[e], b1[e], w2[e], b2[e]) * cw[:, e, None, None]
            return out
        for l in range(L):
            x = x + _attn(_ln(x, ln1_w[l], ln1_b[l]), wq[l], wk[l], wv[l], wo[l], bq[l], bk[l], bv[l], bo[l])
            h = _ln(x, ln2_w[l], ln2_b[l])
            moe = _token_moe if l % 2 == 0 else _seq_moe
            x = x + moe(h, gate_w[l], gate_b[l], e_w1[l], e_b1[l], e_w2[l], e_b2[l])
        return x
    x = _layernorm(x + _L0_attn_ref(x, L0_attn_Wq, L0_attn_bq, L0_attn_Wk, L0_attn_bk, L0_attn_Wv, L0_attn_bv, L0_attn_gamma, L0_attn_beta), axis=-1)
    x = _layernorm(x + _L0_xattn_ref(x, ctx_768, mask_BxS_bk0, L0_xattn_Wq, L0_xattn_Wkv), axis=-1)
    x = _layernorm(x + _L0_ffn_ref(x, L0_ffn_ln1_w, L0_ffn_ln1_b, L0_ffn_ln2_w, L0_ffn_ln2_b, L0_ffn_wq, L0_ffn_wk, L0_ffn_wv, L0_ffn_wo, L0_ffn_bq, L0_ffn_bk, L0_ffn_bv, L0_ffn_bo, L0_ffn_gate_w, L0_ffn_gate_b, L0_ffn_e_w1, L0_ffn_e_b1, L0_ffn_e_w2, L0_ffn_e_b2), axis=-1)
    return x

_drawn_inputs = setup_inputs


def setup_inputs(seed=0):
    import zlib

    import numpy as np

    out = dict(_drawn_inputs(seed))
    spreads = {'L0_attn_bq': (0.0, 0.8),
     'L0_attn_bk': (0.0, 0.8),
     'L0_attn_bv': (0.0, 0.345),
     'L0_attn_gamma': (1.0, 0.2),
     'L0_attn_beta': (0.0, 0.1),
     'L0_ffn_ln1_w': (1.0, 0.6),
     'L0_ffn_ln1_b': (0.0, 0.8),
     'L0_ffn_ln2_w': (1.0, 0.6),
     'L0_ffn_ln2_b': (0.0, 0.479),
     'L0_ffn_bq': (0.0, 0.8),
     'L0_ffn_bk': (0.0, 0.8),
     'L0_ffn_bv': (0.0, 0.397),
     'L0_ffn_bo': (0.0, 0.1),
     'L0_ffn_gate_b': (0.0, 0.1),
     'L0_ffn_e_b1': (0.0, 0.694),
     'L0_ffn_e_b2': (0.0, 0.1)}
    factors = {'L0_attn_Wq': 3.037, 'L0_ffn_wq': 8.0, 'L0_ffn_wk': 8.0, 'L0_ffn_wv': 2.787}
    for name, (base, spread) in spreads.items():
        noise = np.random.default_rng([zlib.crc32(name.encode()), seed]).standard_normal(out[name].shape)
        drawn = base * np.exp(spread * noise) if base else spread * noise
        out[name] = jnp.asarray(drawn.astype(out[name].dtype))
    for name, factor in factors.items():
        out[name] = (out[name] * factor).astype(out[name].dtype)
    return out
```

```python
from contextlib import ExitStack

import numpy as np

import concourse.bass as bass
from concourse import mybir

ALU = mybir.AluOpType
ACT = mybir.ActivationFunctionType
AX = mybir.AxisListType
F32 = mybir.dt.float32
F32R = mybir.dt.float32r
BF16 = mybir.dt.bfloat16
U8 = mybir.dt.uint8
U32 = mybir.dt.uint32

P = 128
B = 16
T = 256
NT = T // P
C = 128
H = 16
DH = C // H
S4 = 4
TC = 64
CC = 96
E = 8
FF = 512
FC = FF // P
K2 = 2
MROW = 3 * 32
MREND = MROW + 8
PASSES = B // 2
SCALE = float(DH) ** -0.5
BIG = float(2 ** 32)
HIDE = -1.0e30


class Signal:

    def __init__(self, sem, lane):
        self.sem, self.lane, self.base, self.per = sem, lane, 0, 0

    def begin(self, per):
        self.base += PASSES * self.per
        self.per = per

    def at(self, n):
        return self.lane.p * self.per + (self.base + n)


class Lane:

    def __init__(self, name, ctx, nc):
        self.name, self.ctx, self.nc = name, ctx, nc
        self.p = 0
        self.first = True
        self.sig = {}
        self.loaded = self.counted("loaded")
        self.tok_ready = self.counted("tok_ready")
        self.transposed = self.counted("transposed")
        self.src_ready = self.counted("src_ready")
        self.projected = self.counted("projected")
        self.qkv_taken = self.counted("qkv_taken")
        self.split_ready = self.counted("split_ready")
        self.stack_ready = self.counted("stack_ready")
        self.scores_ready = self.counted("scores_ready")
        self.max_taken = self.counted("max_taken")
        self.maxparts_ready = self.counted("maxparts_ready")
        self.maxT_ready = self.counted("maxT_ready")
        self.maxT_taken = self.counted("maxT_taken")
        self.maxrows_ready = self.counted("maxrows_ready")
        self.st_ready = self.counted("st_ready")
        self.exp_done = self.counted("exp_done")
        self.masked = self.counted("masked")
        self.pv_done = self.counted("pv_done")
        self.o_taken = self.counted("o_taken")
        self.oT_ready = self.counted("oT_ready")
        self.ao_ready = self.counted("ao_ready")
        self.aoT_ready = self.counted("aoT_ready")
        self.aoT_taken = self.counted("aoT_taken")
        self.y_ready = self.counted("y_ready")
        self.x2_ready = self.counted("x2_ready")
        self.x2_stored = self.counted("x2_stored")
        self.res_ready = self.counted("res_ready")
        self.res_stored = self.counted("res_stored")
        self.ln_var = self.counted("ln_var")
        self.ln_rstd = self.counted("ln_rstd")
        self.dve_step = self.counted("dve_step")
        self.gate_ready = self.counted("gate_ready")
        self.gate_diff = self.counted("gate_diff")
        self.gate_w = self.counted("gate_w")
        self.hidden_ready = self.counted("hidden_ready")
        self.gelu_done = self.counted("gelu_done")
        self.expert_y = self.counted("expert_y")
        self.acc_done = self.counted("acc_done")
        self.expert_chosen = self.counted("expert_chosen")
        self.expert_loaded = self.counted("expert_loaded")
        self.gate_row = self.counted("gate_row")
        self.gate_bcast = self.counted("gate_bcast")
        self.steps = {"dve": 0, "pool": 0}
        self.split_steps = {"dve": 0, "pool": 0}

    def counted(self, name):
        signal = Signal(self.ctx.enter_context(self.nc.semaphore(f"{self.name}_{name}")), self)
        self.sig[name] = signal
        return signal

    def begin_phase(self, per):
        for s, signal in self.sig.items():
            signal.begin(per.get(s, 0))

    def sb(self, name, shape, dtype=F32):
        return self.ctx.enter_context(self.nc.sbuf_tensor(f"{self.phase}_{self.name}_{name}", shape, dtype))


SELF_ROUNDS = [(0, s, None) for s in range(S4)] + [(1, s, u) for s in range(S4) for u in range(2)]
N_SELF = len(SELF_ROUNDS)
N_CTX = 4


class Unit:

    def __init__(self, kind, index, rounds_before, pv_before, masks_before, stack_before, wq, wk, wv,
                 wo=None, bq=None, bk=None, bk2=None, bv2=None, bo2=None, ln_w=None, ln_b=None):
        self.kind, self.u = kind, index
        self.rounds = N_CTX if kind == "ctx" else N_SELF
        self.before, self.pv_before, self.masks_before = rounds_before, pv_before, masks_before
        self.stack_before = stack_before
        self.wq, self.wk, self.wv, self.wo = wq, wk, wv, wo
        self.bq, self.bk, self.bk2, self.bv2, self.bo2 = bq, bk, bk2, bv2, bo2
        self.ln_w, self.ln_b = ln_w, ln_b


def decoder(nc, ins, out):
    top = ExitStack()
    with top:
        sem_setup_dma = top.enter_context(nc.semaphore("setup_loaded"))
        sem_setup = top.enter_context(nc.semaphore("setup_step"))
        sem_setup_pool = top.enter_context(nc.semaphore("setup_pool_step"))
        lanes = [Lane(n, top, nc) for n in ("even", "odd")]
        held_dve, held_pool, held_sp = (top.enter_context(nc.semaphore(f"held_{e}")) for e in ("dve", "pool", "sp"))

        for L in lanes:
            def bank(n):
                return top.enter_context(nc.psum_tensor(f"{L.name}_{n}", [P, 512], F32))
            L.R = [bank("round0"), bank("round1")]
            L.OB = bank("values")
            L.M = bank("mixed")

        def const(name, shape, dtype=F32):
            return top.enter_context(nc.sbuf_tensor(name, shape, dtype))

        ident = const("ident", [P, P])
        ones2 = const("ones2", [2, P], F32R)
        scratch_x2 = [nc.dram_tensor(f"scratch_x2_{n}", [PASSES, P, NT, C], F32).ap() for n in range(2)]
        scratch_a = [nc.dram_tensor(f"scratch_a_{n}", [PASSES, P, NT, C], F32).ap() for n in range(2)]
        scratch_b = [nc.dram_tensor(f"scratch_b_{n}", [PASSES, P, NT, C], F32).ap() for n in range(2)]

        def token_major(dram, lane, p):
            pairs = dram.rearrange("(p l) (n t) c -> l p t n c", l=2, t=P)
            return pairs[lane][bass.ds(p, 1)].rearrange("o t n c -> t (o n) c")

        def scratch(drams, lane, p):
            return drams[lane][bass.ds(p, 1)].rearrange("o t n c -> t (o n) c")


        def link(L, dve, instruction, apart=False):
            L.steps["dve"] += 1
            instruction.then_inc(L.dve_step.sem, 1)
            if apart:
                dve.wait_ge(L.dve_step.sem, L.dve_step.at(L.steps["dve"]))
                dve.sem_inc(held_dve, 1)
            else:
                dve.wait_ge(L.dve_step.sem, L.dve_step.at(L.steps["dve"]))

        def dve_layer_norm(L, dve, z, n, eps, normed):
            for t in range(NT):
                i = dve.bn_stats(L.stats[:, t, :], z[:, t, :])
            link(L, dve, i, apart=True)
            for t in range(NT):
                i = dve.bn_aggr(L.meanvar[:, t, :], L.stats[:, t, :])
            link(L, dve, i)
            dve.tensor_scalar(L.vareps[:], L.meanvar[:, :, 1], eps, None, ALU.add).then_inc(L.ln_var.sem, 1)
            yield
            yield
            dve.wait_ge(L.ln_rstd.sem, L.ln_rstd.at(n + 1))
            for t in range(NT):
                i = dve.tensor_scalar(normed[:, t, :], z[:, t, :], L.meanvar[:, t, 0:1], L.rstd[:, t:t + 1],
                                      ALU.subtract, ALU.mult)
            link(L, dve, i)

        def pool_layer_norm(L, pool, n):
            yield
            pool.wait_ge(L.ln_var.sem, L.ln_var.at(n + 1))
            pool.tensor_tensor(L.rstd[:], L.vareps[:], minus_half[:], ALU.pow).then_inc(L.ln_rstd.sem, 1)
            yield

        minus_half = const("minus_half", [P, NT])


        def pe_scores(L, pe, U):
            u = U.u
            pe.wait_ge(L.tok_ready.sem, L.tok_ready.at(u + 1))
            for t in range(NT):
                i = pe.transpose(L.M[:, t * P:(t + 1) * P], L.tok[:, t, :], ident[:])
            if U.kind == "self":
                for t in range(NT):
                    i = pe.transpose(L.M[0:2, T + t * P:T + (t + 1) * P], L.keep2[:, t, :], ident[:])
            i.then_inc(L.transposed.sem, 1)
            yield
            pe.wait_ge(L.src_ready.sem, L.src_ready.at(u + 1))
            pe.matmul(L.M[:, 0:T], U.wq[:], L.srcT[:], start=True, stop=True)
            if U.kind == "ctx":
                pe.matmul(L.M[:, T:T + TC], U.wk[:], L.ctxT[:, 0:TC], start=True, stop=True)
                i = pe.matmul(L.R[0][:, 0:C], L.ctxT[:], U.wv[:], start=True, stop=True)
            else:
                pe.matmul(L.M[:, T:2 * T], U.wk[:], L.srcT[:], start=True, stop=U.kind != "self")
                if U.kind == "self":
                    pe.matmul(L.M[:, T:2 * T], U.bk2[:], L.keeprows[:], start=False, stop=True)
                for t in range(NT):
                    cols = slice(t * C, (t + 1) * C)
                    pe.matmul(L.R[0][:, cols], L.srcT[:, t * P:(t + 1) * P], U.wv[:], start=True, stop=False)
                    i = pe.matmul(L.R[0][:, cols], ones2[:], U.bv2[:], start=False, stop=True)
            i.then_inc(L.projected.sem, 1)
            yield
            yield
            yield
            yield
            for r in range(U.rounds):
                if r == 0:
                    pe.wait_ge(L.stack_ready.sem, L.stack_ready.at(U.stack_before + 16 * 15))
                if r >= 2:
                    pe.wait_ge(L.max_taken.sem, L.max_taken.at(U.before + r - 1))
                bank = L.R[r % 2]
                if U.kind == "ctx":
                    t = r // 2
                    for k in range(2):
                        s = 2 * (r % 2) + k
                        i = pe.matmul(bank[:, k * 256:(k + 1) * 256], L.Q[0:MROW, s, t * P:(t + 1) * P],
                                      L.KX[0:MROW, 2 * s:2 * s + 2, :].rearrange("p a k -> p (a k)"),
                                      start=True, stop=True)
                else:
                    t, s, half = SELF_ROUNDS[r]
                    if t == 0:
                        pe.matmul(bank[:], L.Q[0:MROW, s, 0:P], L.K[0:MROW, 4 * s:4 * s + 4, 0:P],
                                  start=True, stop=False)
                        i = pe.matmul(bank[:], ident_bf[:], hide[:, None, :].to_broadcast([P, 4, P]),
                                      start=False, stop=True)
                    else:
                        pe.matmul(bank[:], L.Q[0:MROW, s, P:T], L.K[0:MROW, 4 * s + 2 * half:4 * s + 2 * half + 2, :],
                                  start=True, stop=False)
                        i = pe.matmul(bank[:].rearrange("p (h k) -> p h k", h=2)[:, :, P:T], ident_bf[:],
                                      hide[:, None, :].to_broadcast([P, 2, P]), start=False, stop=True)
                i.then_inc(L.scores_ready.sem, 1)
                yield

        def act_scores(L, act, U):
            u = U.u
            act.wait_ge(L.transposed.sem, L.transposed.at(u + 1))
            if U.kind == "self":
                act.copy(L.keeprows[:], L.M[0:2, T:2 * T])
            if U.kind == "ffn":
                i = act.activation(L.srcT[:], L.M[:, 0:T], ACT.Identity, bias=U.ln_b[:], scale=U.ln_w[:])
            else:
                i = act.copy(L.srcT[:], L.M[:, 0:T])
            i.then_inc(L.src_ready.sem, 1)
            yield
            act.wait_ge(L.projected.sem, L.projected.at(u + 1))
            func = ACT.Relu if U.kind == "self" else ACT.Identity
            if U.kind == "ctx":
                for k in range(2):
                    rows = slice(k * TC, (k + 1) * TC)
                    act.copy(L.VX[rows, :, 16 * k:16 * k + DH],
                             L.R[0][rows, 0:C].rearrange("p (n k d) -> p n k d", k=2, d=DH)[:, :, k, :])
                act.copy(L.QK[:, 0:T], L.M[:, 0:T])
                i = act.copy(L.QK[:, T:T + TC], L.M[:, T:T + TC])
            else:
                act.activation(L.V[:, :, :, 0:DH], L.R[0][:, 0:NT * C].rearrange("p (n h d) -> p n h d", n=NT, d=DH),
                               func)
                act.activation(L.QK[:, 0:T], L.M[:, 0:T], func, bias=U.bq[:])
                if U.kind == "self":
                    i = act.activation(L.QK[:, T:2 * T], L.M[:, T:2 * T], func)
                else:
                    i = act.activation(L.QK[:, T:2 * T], L.M[:, T:2 * T], func, bias=U.bk[:])
            i.then_inc(L.qkv_taken.sem, 1)
            yield
            yield
            yield
            yield
            for r in range(U.rounds):
                yield

        def dve_scores(L, dve, U):
            yield
            yield
            dve.wait_ge(L.qkv_taken.sem, L.qkv_taken.at(U.u + 1))
            n = T + (TC if U.kind == "ctx" else T)
            link(L, dve, dve.tensor_copy(L.HI[:, 0:n], L.QK[:, 0:n]))
            dve.tensor_tensor(L.LO[:, 0:n], L.QK[:, 0:n], L.HI[:, 0:n].bitcast(F32),
                              ALU.subtract).then_inc(L.split_ready.sem, 1)
            yield
            yield
            yield
            for r in range(U.rounds):
                dve.wait_ge(L.scores_ready.sem, L.scores_ready.at(U.before + r + 1))
                bank = L.R[r % 2]
                if U.kind == "ctx":
                    t, s0 = r // 2, 2 * (r % 2)
                    for k in range(2):
                        i = dve.tensor_reduce(L.negmax[:, t, :, s0 + k],
                                              bank[:, k * 256:(k + 1) * 256].rearrange("p (a k) -> p a k", a=4),
                                              AX.X, ALU.max, negate=True)
                else:
                    t, s, half = SELF_ROUNDS[r]
                    heads = slice(0, 4) if t == 0 else slice(2 * half, 2 * half + 2)
                    i = dve.tensor_reduce(L.negmax[:, t, heads, s],
                                          bank[:].rearrange("p (a k) -> p a k", k=P * (t + 1)),
                                          AX.X, ALU.max, negate=True)
                i.then_inc(L.max_taken.sem, 1)
                yield

        def sp_scores(L, sp, U):
            yield
            yield
            yield
            sp.wait_ge(L.split_ready.sem, L.split_ready.at(U.u + 1))
            for part, src in enumerate((L.HI, L.HI, L.LO)):
                sp.dma_start(L.Q[32 * part:32 * part + 32, :, :].bitcast(F32), src[:, 0:T].bitcast(F32)).then_inc(L.stack_ready.sem, 16)
            for part, src in enumerate((L.HI, L.LO, L.HI)):
                for a in range(S4):
                    rows = slice(32 * part + 8 * a, 32 * part + 8 * a + 8)
                    if U.kind == "ctx":
                        dst = L.KX[rows, a // 2::2, (a % 2) * TC:(a % 2 + 1) * TC]
                        sp.dma_start(dst.bitcast(F32), src[32 * a:32 * a + 32, T:T + TC].bitcast(F32)).then_inc(L.stack_ready.sem, 16)
                    else:
                        sp.dma_start(L.K[rows, a::S4, :].bitcast(F32),
                                     src[32 * a:32 * a + 32, T:2 * T].bitcast(F32)).then_inc(L.stack_ready.sem, 16)
            yield
            yield
            for r in range(U.rounds):
                yield

        def pool_scores(L, pool, U):
            for r in range(5 + U.rounds):
                yield


        def pe_values(L, pe, U):
            u = U.u
            pe.wait_ge(L.maxparts_ready.sem, L.maxparts_ready.at(u + 1))
            for t in range(NT):
                i = pe.transpose(L.M[0:32, t * P:(t + 1) * P],
                                 L.maxparts[:, t, :, :].rearrange("p r h -> p (r h)").bitcast(F32), ident[:])
            i.then_inc(L.maxT_ready.sem, 1)
            yield
            yield
            yield
            yield

            def first_keys(s):
                pe.wait_ge(L.masked.sem, L.masked.at(U.masks_before + 6 * (s // 2) + 2 * (s % 2) + 2))
                if s == 2:
                    pe.wait_ge(L.o_taken.sem, L.o_taken.at(U.pv_before + 1))
                for a in range(S4):
                    r = 6 * (s // 2) + 2 * (s % 2) + a // 2
                    pe.matmul(L.OB[32 * a:32 * a + 32, (s % 2) * T:(s % 2 + 1) * T], L.V[:, 0, 4 * s + a, :],
                              L.probs[:, r, (a % 2) * T:(a % 2 + 1) * T], start=(s % 2 == 0), stop=False,
                              tile_position=(0, 32 * a), skip_group_check=True)

            def second_keys(pair):
                pe.wait_ge(L.masked.sem, L.masked.at(U.masks_before + 6 * pair + 6))
                for s in (2 * pair, 2 * pair + 1):
                    for a in range(S4):
                        i = pe.matmul(L.OB[32 * a:32 * a + 32, (s % 2) * T + P:(s % 2 + 1) * T], L.V[:, 1, 4 * s + a, :],
                                      L.probs[:, 6 * pair + 4 + s % 2, a * P:(a + 1) * P], start=False,
                                      stop=True, tile_position=(0, 32 * a), skip_group_check=True)
                i.then_inc(L.pv_done.sem, 1)

            for r in range(U.rounds):
                if r == 0:
                    pe.wait_ge(L.maxrows_ready.sem, L.maxrows_ready.at(16 * (u + 1)))
                if r >= 2:
                    pe.wait_ge(L.exp_done.sem, L.exp_done.at(U.before + r - 1))
                bank = L.R[r % 2]
                if U.kind == "ctx":
                    for k in range(2):
                        i = pe.matmul(bank[:, k * T:(k + 1) * T], L.KX[0:MREND, 2 * r + k, :], L.Q[0:MREND, r, :],
                                      start=True, stop=True)
                    i.then_inc(L.st_ready.sem, 1)
                    if r >= 2:
                        context_values(L, pe, U, r - 2)
                else:
                    pair, j = divmod(r, 6)
                    if j < 4:
                        s = 2 * pair + j // 2
                        for k in range(2):
                            i = pe.matmul(bank[:, k * T:(k + 1) * T], L.K[0:MREND, 4 * s + 2 * (j % 2) + k, 0:P],
                                          L.Q[0:MREND, s, :], start=True, stop=True)
                    else:
                        s = 2 * pair + j - 4
                        for a in range(S4):
                            i = pe.matmul(bank[:, a * P:(a + 1) * P], L.K[0:MREND, 4 * s + a, P:T],
                                          L.Q[0:MREND, s, P:T], start=True, stop=True)
                    i.then_inc(L.st_ready.sem, 1)
                    if j == 3:
                        first_keys(2 * pair)
                    if j == 5:
                        first_keys(2 * pair + 1)
                    if r == 7:
                        second_keys(0)
                yield
            if U.kind == "ctx":
                context_values(L, pe, U, 2)
                context_values(L, pe, U, 3)
            else:
                second_keys(1)
            yield
            slots = 2 if U.kind == "ctx" else 4
            pe.wait_ge(L.o_taken.sem, L.o_taken.at(U.pv_before + (1 if U.kind == "ctx" else 2)))
            for t in range(NT):
                to = (L.M, L.R[0])[t]
                for s in range(slots):
                    i = pe.transpose(to[:, s * P:(s + 1) * P],
                                     L.O[:, s // 2, (s % 2) * T + t * P:(s % 2) * T + (t + 1) * P], ident[:])
            i.then_inc(L.oT_ready.sem, 1)
            yield
            yield

        def context_values(L, pe, U, s):
            pe.wait_ge(L.exp_done.sem, L.exp_done.at(U.before + s + 1))
            for k in range(2):
                c = (s % 2) * 2 + k
                i = pe.matmul(L.OB[32 * c:32 * c + 32, (s // 2) * T:(s // 2 + 1) * T], L.VX[:, 2 * s + k, :],
                              L.probs[:, s, k * T:(k + 1) * T], start=True, stop=True, tile_position=(0, 32 * c))
            if s == S4 - 1:
                i.then_inc(L.pv_done.sem, 1)

        def act_values(L, act, U):
            u = U.u
            yield
            act.wait_ge(L.maxT_ready.sem, L.maxT_ready.at(u + 1))
            act.copy(L.maxT[:], L.M[0:32, 0:T]).then_inc(L.maxT_taken.sem, 1)
            yield
            yield
            yield

            def take_outputs(half):
                act.wait_ge(L.pv_done.sem, L.pv_done.at(U.pv_before + half + 1))
                act.copy(L.O[:, half, :], L.OB[:]).then_inc(L.o_taken.sem, 1)

            for r in range(U.rounds):
                act.wait_ge(L.st_ready.sem, L.st_ready.at(U.before + r + 1))
                bias = {}
                if U.kind == "self":
                    bias["bias"] = L.keybias[:, 0:1] if r % 6 < 4 else L.keybias[:, 1:2]
                act.activation(L.probs[:, r, :], L.R[r % 2][:], ACT.Exp, scale=SCALE,
                               **bias).then_inc(L.exp_done.sem, 1)
                if U.kind != "ctx" and r == 8:
                    take_outputs(0)
                yield
            take_outputs(0 if U.kind == "ctx" else 1)
            yield
            yield
            yield

        def pool_values(L, pool, U):
            for _ in range(4):
                yield
            for r in range(U.rounds):
                if U.kind != "ctx":
                    pool.wait_ge(L.exp_done.sem, L.exp_done.at(U.before + r + 1))
                    pool.sem_inc(held_pool, 1)
                    heads, width = (2, T) if r % 6 < 4 else (4, P)
                    block = L.probs[:, r, :].rearrange("p (h q) -> p h q", h=heads)[:, :, 0:P]
                    pool.affine_select(out=block, in_=block, compare_op=ALU.is_ge, fill=0.0, base=0,
                                       pattern=[[0, heads], [1, P]], channel_multiplier=-1).then_inc(L.masked.sem, 1)
                yield
            for _ in range(3):
                yield

        def dve_values(L, dve, U):
            dve.wait_ge(L.max_taken.sem, L.max_taken.at(U.before + U.rounds))
            flat = L.negmax[:].rearrange("p t a s -> p t (a s)")
            link(L, dve, dve.tensor_copy(L.maxparts[:, :, 0, :], flat))
            dve.tensor_tensor(L.maxparts[:, :, 1, :], flat, L.maxparts[:, :, 0, :].bitcast(F32),
                              ALU.subtract).then_inc(L.maxparts_ready.sem, 1)
            for _ in range(4 + U.rounds):
                yield
            yield
            yield
            dve.wait_ge(L.oT_ready.sem, L.oT_ready.at(U.u + 1))
            w = 16 if U.kind == "ctx" else 32
            for t in range(NT):
                o = (L.M, L.R[0])[t][:, 0:H * w].rearrange("p (h r) -> p h r", r=w)
                if U.kind == "self":
                    i = dve.tensor_scalar(L.denom[:, t, :], o[:, :, DH], 1e-30, None, ALU.max)
                else:
                    i = dve.tensor_copy(L.denom[:, t, :], o[:, :, DH])
            link(L, dve, i)
            link(L, dve, dve.reciprocal(L.denom[:], L.denom[:]))
            for t in range(NT):
                o = (L.M, L.R[0])[t][:, 0:H * w].rearrange("p (h r) -> p h r", r=w)
                i = dve.tensor_tensor(L.AO[:, t, :].rearrange("p (h d) -> p h d", d=DH), o[:, :, 0:DH],
                                      L.denom[:, t, :, None].to_broadcast([P, H, DH]), ALU.mult)
            if U.kind == "ffn":
                i.then_inc(L.ao_ready.sem, 1)
            else:
                link(L, dve, i)
            yield

        def sp_values(L, sp, U):
            yield
            yield
            sp.wait_ge(L.maxT_taken.sem, L.maxT_taken.at(U.u + 1))
            sp.dma_start(L.Q[MROW:MREND, :, :].bitcast(F32), L.maxT[:].bitcast(F32)).then_inc(L.maxrows_ready.sem, 16)
            yield
            yield
            for r in range(U.rounds):
                yield
            yield
            yield
            yield


        def pe_project(L, pe, U):
            pe.wait_ge(L.ao_ready.sem, L.ao_ready.at(1))
            for t in range(NT):
                i = pe.transpose(L.M[:, t * P:(t + 1) * P], L.AO[:, t, :], ident[:])
            i.then_inc(L.aoT_ready.sem, 1)
            yield
            yield
            pe.wait_ge(L.aoT_taken.sem, L.aoT_taken.at(1))
            for t in range(NT):
                cols = slice(t * C, (t + 1) * C)
                pe.matmul(L.OB[:, cols], L.aoT[:, t * P:(t + 1) * P], U.wo[:], start=True, stop=False)
                i = pe.matmul(L.OB[:, cols], ones2[:], U.bo2[:], start=False, stop=True)
            i.then_inc(L.y_ready.sem, 1)
            yield
            yield

        def act_project(L, act, U):
            yield
            act.wait_ge(L.aoT_ready.sem, L.aoT_ready.at(1))
            act.copy(L.aoT[:], L.M[:, 0:T]).then_inc(L.aoT_taken.sem, 1)
            yield
            yield
            yield

        def dve_project(L, dve, U):
            yield
            yield
            yield
            dve.wait_ge(L.y_ready.sem, L.y_ready.at(1))
            if not L.first:
                dve.wait_ge(L.res_stored.sem, L.res_stored.at(0))
            dve.tensor_tensor(L.res[:], L.resid[:], L.OB[:, 0:NT * C].rearrange("p (t c) -> p t c", t=NT),
                              ALU.add).then_inc(L.res_ready.sem, 1)
            yield

        def sp_project(L, sp, U, to):
            yield
            yield
            yield
            yield



        def run(eng, head, tail, which):

            even, odd = lanes

            def turn(p, first):
                even.p = p
                even.first = first
                even.steps = {"dve": 0, "pool": 0}

                def evens():
                    yield from head(even, eng)
                    yield from tail(even, eng)

                def odds():
                    if not first:
                        odd.p, odd.first = p - 1, False
                        odd.steps = dict(odd.split_steps)
                        yield from tail(odd, eng)
                    odd.p, odd.first = p, first
                    odd.steps = {"dve": 0, "pool": 0}
                    yield from head(odd, eng)
                    odd.split_steps = dict(odd.steps)

                together(evens(), odds())

            turn(0, True)
            with eng.Fori(1, PASSES) as p:
                turn(p, False)
            even.p = odd.p = PASSES - 1
            odd.steps = dict(odd.split_steps)
            for _ in tail(odd, eng):
                pass
            if which == "dve":
                for L in lanes:
                    if L.steps["dve"] != L.dve_step.per:
                        raise ValueError(f"dve_step makes {L.steps['dve']} in a pass, not {L.dve_step.per}")

        def together(one, two):
            live = [one, two]
            while live:
                for g in list(live):
                    try:
                        next(g)
                    except StopIteration:
                        live.remove(g)

        ident_bf = const("ident_bf", [P, P], BF16)
        hide = const("hide", [P, P], BF16)
        with nc.Block() as block:
            @block.gpsimd
            def _(pool):
                pool.memset(ident[:], 0.0)
                pool.memset(hide[:], 0.0)
                pool.memset(minus_half[:], -0.5).then_inc(sem_setup_pool, 1)
                pool.wait_ge(sem_setup_pool, 1)
                pool.affine_select(out=ident[:], in_=ident[:], compare_op=ALU.not_equal, fill=1.0, base=0,
                                   pattern=[[-1, P]], channel_multiplier=1).then_inc(sem_setup_pool, 1)
                pool.affine_select(out=hide[:], in_=hide[:], compare_op=ALU.is_ge, fill=HIDE, base=0,
                                   pattern=[[-1, P]], channel_multiplier=1).then_inc(sem_setup_pool, 1)

            @block.vector
            def _(dve):
                dve.wait_ge(sem_setup_pool, 3)
                dve.tensor_copy(ident_bf[:], ident[:]).then_inc(sem_setup, 1)
                dve.memset(ones2[:].bitcast(F32), 1.0).then_inc(sem_setup, 1)
                dve.wait_ge(sem_setup, 2)
        setup_count = {"dma": 0, "dve": 2, "pool": 3}

        def load_block(pairs, splits, extra_pool=None, extra_dve=None):
            base = dict(setup_count)
            with nc.Block() as block:
                @block.sync
                def _(sp):
                    for dst, src in pairs:
                        sp.dma_start(dst, src).then_inc(sem_setup_dma, 16)
                    sp.wait_ge(sem_setup_dma, base["dma"] + 16 * len(pairs))
                    if splits:
                        sp.wait_ge(sem_setup, base["dve"] + 2)
                        for rows, _, low in splits:
                            sp.dma_start(rows[1:2, :].bitcast(F32), low[:].bitcast(F32)).then_inc(sem_setup_dma, 16)
                        sp.wait_ge(sem_setup_dma, base["dma"] + 16 * (len(pairs) + len(splits)))

                @block.vector
                def _(dve):
                    if splits:
                        dve.wait_ge(sem_setup_dma, base["dma"] + 16 * len(pairs))
                        for rows, raw, _ in splits:
                            i = dve.tensor_copy(rows[0:1, :], raw[:])
                        i.then_inc(sem_setup, 1)
                        dve.wait_ge(sem_setup, base["dve"] + 1)
                        for rows, raw, low in splits:
                            i = dve.tensor_tensor(low[:], raw[:], rows[0:1, :].bitcast(F32), ALU.subtract)
                        i.then_inc(sem_setup, 1)
                        dve.wait_ge(sem_setup, base["dve"] + 2)
                    if extra_dve:
                        extra_dve(dve, base)

                @block.gpsimd
                def _(pool):
                    if extra_pool:
                        extra_pool(pool, base)
            setup_count["dma"] += 16 * (len(pairs) + len(splits))
            if splits:
                setup_count["dve"] += 2

        def lane_attention_buffers(with_ctx):
            for L in lanes:
                L.Q = L.sb("queries", [P, S4, T], F32R)
                L.K = L.sb("keys", [P, H, T], F32R)
                L.V = L.sb("v", [P, NT, H, 32])
                L.probs = L.sb("probs", [P, N_SELF, 512])
                L.QK = L.sb("qk", [P, 2 * T])
                L.HI = L.sb("hi", [P, 2 * T], F32R)
                L.LO = L.sb("lo", [P, 2 * T], F32R)
                L.negmax = L.sb("negmax", [P, NT, S4, S4])
                L.maxparts = L.sb("maxparts", [P, NT, 2, H], F32R)
                L.maxT = L.sb("maxT", [32, T], F32R)
                L.O = L.sb("o", [P, 2, 512])
                L.AO = L.sb("ao", [P, NT, C])
                L.aoT = L.sb("aoT", [P, T])
                L.srcT = L.sb("srcT", [P, T])
                L.denom = L.sb("denom", [P, NT, H])
                if with_ctx:
                    L.KX = L.sb("ctx_keys", [P, H // 2, 2 * TC], F32R)
                    L.VX = L.sb("ctx_v", [P, H // 2, 32])
                    L.ctxT = L.sb("ctxT", [CC, 2 * TC])

        def lane_common_buffers():
            for L in lanes:
                L.tok = L.sb("tok", [P, NT, C])
                L.x = L.sb("x", [P, NT, C])
                L.res = L.sb("res", [P, NT, C])
                L.stats = L.sb("stats", [P, NT, 6])
                L.meanvar = L.sb("meanvar", [P, NT, 2])
                L.vareps = L.sb("vareps", [P, NT])
                L.rstd = L.sb("rstd", [P, NT])

        def stack_image(L):
            flat = L.probs[:].rearrange("p r n -> p (r n)")
            return (flat[:, 0:H * T].rearrange("p (h k) -> p h k", h=H),
                    flat[:, H * T:H * T + H * TC].rearrange("p (i k) -> p i k", i=H // 2))

        def init_stacks(with_ctx):
            def pool_part(pool, base):
                n = base["pool"]
                for L in lanes:
                    pool.memset(L.probs[:], 0.0)
                    pool.memset(L.Q[:].bitcast(F32), 0.0)
                pool.memset(minus_half[:], -0.5).then_inc(sem_setup_pool, 1)
                n += 1
                for part in range(2):
                    pool.wait_ge(sem_setup_pool, n)
                    for L in lanes:
                        view = stack_image(L)[0][MROW:P].rearrange("p (s a) k -> p s a k", a=S4)
                        for s in range(S4):
                            i = pool.affine_select(out=view[:, s], in_=view[:, s], compare_op=ALU.not_equal, fill=1.0,
                                                   base=-4 * part, pattern=[[-1, S4], [0, T]], channel_multiplier=1)
                        if with_ctx:
                            for s in range(S4):
                                view = stack_image(L)[1][MROW:P, 2 * s:2 * s + 2, :].rearrange(
                                    "p i (h k) -> p (i h) k", h=2)
                                i = pool.affine_select(out=view, in_=view, compare_op=ALU.not_equal, fill=1.0,
                                                       base=-4 * part, pattern=[[-1, S4], [0, TC]],
                                                       channel_multiplier=1)
                    i.then_inc(sem_setup_pool, 1)
                    n += 1
                pool.wait_ge(sem_setup_pool, n)

            def dve_part(dve, base):
                n = base["dve"] + 2
                dve.wait_ge(sem_setup_pool, base["pool"] + 3)
                for L in lanes:
                    keys, ctx_keys = stack_image(L)
                    dve.tensor_copy(L.K[:], keys)
                    if with_ctx:
                        dve.tensor_copy(L.KX[:], ctx_keys)
                for L in lanes:
                    i = dve.memset(L.V[:], 0.0)
                    if with_ctx:
                        i = dve.memset(L.VX[:], 0.0)
                i.then_inc(sem_setup, 1)
                dve.wait_ge(sem_setup, n + 1)
                for L in lanes:
                    i = dve.memset(L.V[:, :, :, DH:DH + 1], 1.0)
                    if with_ctx:
                        for k in range(2):
                            i = dve.memset(L.VX[k * TC:(k + 1) * TC, :, 16 * k + DH:16 * k + DH + 1], 1.0)
                i.then_inc(sem_setup, 1)
                dve.wait_ge(sem_setup, n + 2)
            return pool_part, dve_part

        def row(name, n, ctx):
            return (ctx.enter_context(nc.sbuf_tensor(f"{name}_2", [2, n], F32R)),
                    ctx.enter_context(nc.sbuf_tensor(f"{name}_raw", [1, n], F32)),
                    ctx.enter_context(nc.sbuf_tensor(f"{name}_low", [1, n], F32R)))

        def swap_ctx(ctx, name):
            for L in lanes:
                L.ctx, L.phase = ctx, name

        attention_per_unit = dict(tok_ready=1, transposed=1, src_ready=1, projected=1, qkv_taken=1, split_ready=1,
                                  stack_ready=240, maxparts_ready=1, maxT_ready=1, maxT_taken=1, maxrows_ready=16,
                                  oT_ready=1)
        project_per = dict(ao_ready=1, aoT_ready=1, aoT_taken=1, y_ready=1, res_ready=1, res_stored=16)

        phase = ExitStack()
        with phase:
            swap_ctx(phase, "p1")
            lane_common_buffers()
            lane_attention_buffers(True)
            for L in lanes:
                L.x1 = L.sb("x1", [P, NT, C])
                L.x2 = L.sb("x2", [P, NT, C])
                L.resid = L.x2
                L.keep2 = L.sb("keep2", [P, NT, 2])
                L.keeprows = L.sb("keeprows", [2, T], F32R)
                L.keep = L.sb("keep", [P, NT])
                L.gone = L.sb("gone", [P, NT])
                L.keybias = L.sb("keybias", [P, NT])
                L.sums = L.sb("sums", [P, NT])
                L.pad8 = L.sb("pad8", [P, NT], U8)
                L.pad = L.sb("pad", [P, NT])

            def pt(name, shape, dtype=F32):
                return phase.enter_context(nc.sbuf_tensor(name, shape, dtype))

            w = {}
            pairs, splits = [], []
            for n in ("a_wq", "a_wk", "a_wv", "x_wq", "l0_wq", "l0_wk", "l0_wv", "l0_wo"):
                w[n] = pt(n, [P, C])
            for n in ("x_wk", "x_wv"):
                w[n] = pt(n, [CC, C])
            for n in ("a_bq", "l0_bq", "l0_bk", "l0_ln1_w", "l0_ln1_b"):
                w[n] = pt(n, [P, 1])
            for n in ("a_gamma", "a_beta"):
                w[n] = pt(n, [P, C])
            for n in w:
                src = ins[n]
                if n in ("a_gamma", "a_beta"):
                    src = src.to_broadcast([P, C])
                pairs.append((w[n][:], src))
            for n in ("a_bk", "a_bv", "l0_bv", "l0_bo"):
                w[n + "2"], raw, low = row(n, C, phase)
                pairs.append((raw[:], ins[n]))
                splits.append((w[n + "2"], raw, low))
            pool_part, dve_part = init_stacks(True)
            load_block(pairs, splits, pool_part, dve_part)
            setup_count["pool"] += 3
            setup_count["dve"] += 2

            A = Unit("self", 0, 0, 0, 0, wq=w["a_wq"], wk=w["a_wk"], wv=w["a_wv"], bq=w["a_bq"], bk2=w["a_bk2"],
                     bv2=w["a_bv2"], stack_before=0)
            X = Unit("ctx", 1, N_SELF, 2, N_SELF, wq=w["x_wq"], wk=w["x_wk"], wv=w["x_wv"], stack_before=240)
            F0 = Unit("ffn", 2, N_SELF + N_CTX, 3, N_SELF, wq=w["l0_wq"], wk=w["l0_wk"], wv=w["l0_wv"], wo=w["l0_wo"],
                      bq=w["l0_bq"], bk=w["l0_bk"], bv2=w["l0_bv2"], bo2=w["l0_bo2"], ln_w=w["l0_ln1_w"],
                      ln_b=w["l0_ln1_b"], stack_before=480)
            per = {k: 3 * v for k, v in attention_per_unit.items()} | project_per
            rounds = 2 * N_SELF + N_CTX
            per |= dict(scores_ready=rounds, max_taken=rounds, st_ready=rounds, exp_done=rounds, masked=2 * N_SELF,
                        pv_done=5, o_taken=5, loaded=64, x2_ready=1, x2_stored=16, ln_var=4, ln_rstd=4,
                        dve_step=34)
            for L in lanes:
                L.begin_phase(per)

            def dve_head(L, dve):
                for _ in range(3):
                    yield
                dve.wait_ge(L.loaded.sem, L.loaded.at(64))
                dve.tensor_copy(L.pad[:], L.pad8[:])
                link(L, dve, dve.tensor_reduce(L.sums[:], L.x[:], AX.X, ALU.add))
                link(L, dve, dve.tensor_scalar(L.gone[:], L.sums[:], 0.0, None, ALU.is_equal))
                dve.tensor_scalar(L.keybias[:], L.gone[:], -BIG, None, ALU.mult)
                dve.tensor_scalar(L.keep2[:], L.gone[:, :, None].to_broadcast([P, NT, 2]), -1.0, 1.0, ALU.mult, ALU.add)
                link(L, dve, dve.tensor_scalar(L.keep[:], L.gone[:], -1.0, 1.0, ALU.mult, ALU.add))
                for t in range(NT):
                    i = dve.tensor_scalar(L.tok[:, t, :], L.x[:, t, :], L.keep[:, t:t + 1], None, ALU.mult)
                i.then_inc(L.tok_ready.sem, 1)
                yield
                yield from dve_scores(L, dve, A)
                yield from dve_values(L, dve, A)
                for t in range(NT):
                    i = dve.scalar_tensor_tensor(L.res[:, t, :], L.AO[:, t, :], L.keep[:, t:t + 1], L.x[:, t, :],
                                                 ALU.mult, ALU.add)
                link(L, dve, i)
                yield from dve_layer_norm(L, dve, L.res, 0, 1e-8, L.x1)
                gamma, beta = (w[n][:, None, :].to_broadcast([P, NT, C]) for n in ("a_gamma", "a_beta"))
                link(L, dve, dve.tensor_tensor(L.x1[:], L.x1[:], gamma, ALU.mult))
                link(L, dve, dve.tensor_tensor(L.x1[:], L.x1[:], beta, ALU.add))
                link(L, dve, dve.tensor_tensor(L.res[:], L.x1[:], L.x[:], ALU.add))
                yield from dve_layer_norm(L, dve, L.res, 1, 1e-5, L.x1)
                for t in range(NT):
                    i = dve.tensor_scalar(L.tok[:, t, :], L.x1[:, t, :], L.pad[:, t:t + 1], None, ALU.mult)
                i.then_inc(L.tok_ready.sem, 1)
                yield
                yield from dve_scores(L, dve, X)
                yield from dve_values(L, dve, X)
                link(L, dve, dve.tensor_tensor(L.res[:], L.AO[:], L.x1[:], ALU.add))
                if not L.first:
                    dve.wait_ge(L.x2_stored.sem, L.x2_stored.at(0))
                yield from dve_layer_norm(L, dve, L.res, 2, 1e-5, L.x2)
                dve.tensor_copy(L.gone[:], L.keep[:]).then_inc(L.x2_ready.sem, 1)
                yield from dve_layer_norm(L, dve, L.x2, 3, 1e-5, L.tok)
                dve.tensor_copy(L.gone[:], L.keep[:]).then_inc(L.tok_ready.sem, 1)
                yield
                yield from dve_scores(L, dve, F0)

            def dve_tail(L, dve):
                yield from dve_values(L, dve, F0)
                yield from dve_project(L, dve, F0)
                yield
                yield

            def other_head(scores, values, norm):
                def head(L, eng):
                    for _ in range(4):
                        yield
                    yield from scores(L, eng, A)
                    yield from values(L, eng, A)
                    yield from norm(L, eng, 0)
                    yield from norm(L, eng, 1)
                    yield
                    yield from scores(L, eng, X)
                    yield from values(L, eng, X)
                    yield from norm(L, eng, 2)
                    yield from norm(L, eng, 3)
                    yield
                    yield from scores(L, eng, F0)
                return head

            def other_tail(values, project):
                def tail(L, eng):
                    yield from values(L, eng, F0)
                    if project:
                        yield from project(L, eng, F0)
                    else:
                        for _ in range(4):
                            yield
                    yield
                    yield
                return tail

            def idle_norm(L, eng, n):
                yield
                yield

            def sp_head(L, sp):
                lane = lanes.index(L)
                sp.dma_start(L.x[:], token_major(ins["x"], lane, L.p)).then_inc(L.loaded.sem, 16)
                ctx_src = ins["ctxT"].rearrange("(p l) c k -> l p c k", l=2)[lane][bass.ds(L.p, 1)].rearrange(
                    "o c k -> c (o k)")
                for k in range(2):
                    sp.dma_start(L.ctxT[:, k * TC:(k + 1) * TC], ctx_src).then_inc(L.loaded.sem, 16)
                pad_src = ins["pad"].rearrange("(p l) t n -> l p t n", l=2)[lane][bass.ds(L.p, 1)].rearrange(
                    "o t n -> t (o n)")
                sp.dma_start(L.pad8[:], pad_src).then_inc(L.loaded.sem, 16)
                for _ in range(4):
                    yield
                yield from sp_scores(L, sp, A)
                yield from sp_values(L, sp, A)
                yield from idle_norm(L, sp, 0)
                yield from idle_norm(L, sp, 1)
                yield
                yield from sp_scores(L, sp, X)
                yield from sp_values(L, sp, X)
                yield from idle_norm(L, sp, 2)
                sp.wait_ge(L.x2_ready.sem, L.x2_ready.at(1))
                sp.dma_start(scratch(scratch_x2, lane, L.p), L.x2[:]).then_inc(L.x2_stored.sem, 16)
                yield from idle_norm(L, sp, 3)
                yield
                yield from sp_scores(L, sp, F0)

            def sp_tail(L, sp):
                yield from sp_values(L, sp, F0)
                for _ in range(4):
                    yield
                sp.wait_ge(L.res_ready.sem, L.res_ready.at(1))
                sp.dma_start(scratch(scratch_a, lanes.index(L), L.p), L.res[:]).then_inc(L.res_stored.sem, 16)
                yield
                yield

            with nc.Block() as block:
                @block.sync
                def _(sp):
                    run(sp, sp_head, sp_tail, "sp")
                    for L in lanes:
                        sp.wait_ge(L.res_stored.sem, L.res_stored.at(16))
                        sp.wait_ge(L.x2_stored.sem, L.x2_stored.at(16))

                @block.tensor
                def _(pe):
                    run(pe, other_head(pe_scores, pe_values, idle_norm), other_tail(pe_values, pe_project), "pe")

                @block.scalar
                def _(act):
                    run(act, other_head(act_scores, act_values, idle_norm), other_tail(act_values, act_project), "act")

                @block.vector
                def _(dve):
                    run(dve, dve_head, dve_tail, "dve")

                @block.gpsimd
                def _(pool):
                    run(pool, other_head(pool_scores, pool_values, pool_layer_norm), other_tail(pool_values, None),
                        "pool")

        moe_per = dict(loaded=16, tok_ready=1, transposed=1, src_ready=1, res_ready=1, res_stored=16, gate_ready=1)

        def lane_moe_buffers():
            for L in lanes:
                L.hT = L.sb("hT", [P, T])
                L.g = L.sb("g", [P, 2, FC, T])
                L.logits = L.sb("logits", [P, NT, E])
                L.top = L.sb("top", [P, NT, E])
                L.index = L.sb("index", [P, NT, E], U32)
                L.indexf = L.sb("indexf", [P, NT, E])
                L.diff = L.sb("diff", [P, NT])
                L.tanh = L.sb("tanh", [P, NT])
                L.gate2 = L.sb("gate2", [P, NT, K2])
                L.picked = L.sb("picked", [P, NT, K2, E])
                L.cw = L.sb("cw", [P, NT, E])

        def pe_experts(L, pe, n, w1, w2, b2rows, before):
            def outputs(e):
                pe.wait_ge(L.gelu_done.sem, L.gelu_done.at(2 * (e + 1)))
                if e >= 2:
                    pe.wait_ge(L.acc_done.sem, L.acc_done.at(e - 1))
                y = (L.OB, L.M)[e % 2]
                for t in range(NT):
                    for c in range(FC):
                        i = pe.matmul(y[:, t * C:(t + 1) * C], L.g[:, e % 2, c, t * P:(t + 1) * P], w2(e, c),
                                      start=(c == 0), stop=(c == FC - 1 and b2rows is None))
                    if b2rows is not None:
                        i = pe.matmul(y[:, t * C:(t + 1) * C], ones2[:], b2rows(e), start=False, stop=True)
                i.then_inc(L.expert_y.sem, 1)

            for e in range(n):
                before(e)
                for half in range(2):
                    if e >= 1:
                        pe.wait_ge(L.gelu_done.sem, L.gelu_done.at(2 * e - 1 + half))
                    for k in range(2):
                        i = pe.matmul(L.R[half][:, k * T:(k + 1) * T], w1(e, 2 * half + k), L.hT[:],
                                      start=True, stop=True)
                    i.then_inc(L.hidden_ready.sem, 1)
                if e >= 1:
                    outputs(e - 1)
                yield
            outputs(n - 1)
            yield

        def act_experts(L, act, n, b1):
            for e in range(n):
                if e >= 2:
                    act.wait_ge(L.expert_y.sem, L.expert_y.at(e - 1))
                for half in range(2):
                    act.wait_ge(L.hidden_ready.sem, L.hidden_ready.at(2 * e + half + 1))
                    for k in range(2):
                        c = 2 * half + k
                        i = act.activation(L.g[:, e % 2, c, :], L.R[half][:, k * T:(k + 1) * T], ACT.Gelu,
                                           bias=b1(e, c))
                    i.then_inc(L.gelu_done.sem, 1)
                yield
            yield

        phase = ExitStack()
        with phase:
            swap_ctx(phase, "p2")
            lane_common_buffers()
            lane_moe_buffers()

            def pt(name, shape, dtype=F32):
                return phase.enter_context(nc.sbuf_tensor(name, shape, dtype))

            w1 = pt("m0_w1", [P, E, FF])
            w2 = pt("m0_w2", [P, E, FC, C])
            b1 = pt("m0_b1", [P, E, FC])
            gw = pt("m0_gw", [P, E])
            gb = pt("m0_gb", [P, E])
            lnw = pt("m0_lnw", [P, 1])
            lnb = pt("m0_lnb", [P, 1])
            number = pt("m0_number", [P, E])
            b2rows, b2raw, b2low = row("m0_b2", E * C, phase)
            pairs = [(w1[:, e, :], ins["m0_w1"][e]) for e in range(E)]
            pairs += [(w2[:, e], ins["m0_w2"][e]) for e in range(E)]
            pairs += [(b1[:], ins["m0_b1"]), (gw[:], ins["m0_gw"]), (gb[:], ins["m0_gb"].to_broadcast([P, E])),
                      (lnw[:], ins["m0_lnw"]), (lnb[:], ins["m0_lnb"]), (b2raw[:], ins["m0_b2"])]

            def numbers(pool, base):
                pool.iota(number[:], pattern=[[1, E]], base=0, channel_multiplier=0,
                          allow_small_or_imprecise_dtypes=True).then_inc(sem_setup_pool, 1)
                pool.wait_ge(sem_setup_pool, base["pool"] + 1)
            load_block(pairs, [(b2rows, b2raw, b2low)], numbers)
            setup_count["pool"] += 1
            for L in lanes:
                L.begin_phase(moe_per | dict(ln_var=1, ln_rstd=1, gate_diff=1, gate_w=1, hidden_ready=2 * E,
                                             gelu_done=2 * E, expert_y=E, acc_done=E, dve_step=10))

            def dve_head(L, dve):
                yield
                yield
                dve.wait_ge(L.loaded.sem, L.loaded.at(16))
                yield from dve_layer_norm(L, dve, L.x, 0, 1e-5, L.tok)
                dve.tensor_copy(L.diff[:], L.rstd[:]).then_inc(L.tok_ready.sem, 1)
                yield
                yield
                yield
                dve.wait_ge(L.gate_ready.sem, L.gate_ready.at(1))
                link(L, dve, dve.tensor_tensor(L.logits[:], L.OB[:, 0:NT * E].rearrange("p (t e) -> p t e", t=NT),
                                               gb[:, None, :].to_broadcast([P, NT, E]), ALU.add), apart=True)
                for t in range(NT):
                    i = dve.max(L.top[:, t, :], L.logits[:, t, :])
                link(L, dve, i)
                dve.tensor_tensor(L.diff[:], L.top[:, :, 0], L.top[:, :, 1], ALU.subtract).then_inc(L.gate_diff.sem, 1)
                for t in range(NT):
                    i = dve.max_index(L.index[:, t, :], L.top[:, t, :], L.logits[:, t, :])
                link(L, dve, i)
                link(L, dve, dve.tensor_copy(L.indexf[:], L.index[:]))
                yield
                yield
                dve.wait_ge(L.gate_w.sem, L.gate_w.at(1))
                dve.tensor_scalar(L.gate2[:, :, 0], L.tanh[:], 0.5, 0.5, ALU.mult, ALU.add)
                link(L, dve, dve.tensor_scalar(L.gate2[:, :, 1], L.tanh[:], -0.5, 0.5, ALU.mult, ALU.add))
                for t in range(NT):
                    for k in range(K2):
                        i = dve.tensor_scalar(L.picked[:, t, k, :], number[:], L.indexf[:, t, k:k + 1],
                                              L.gate2[:, t, k:k + 1], ALU.is_equal, ALU.mult)
                link(L, dve, i)
                link(L, dve, dve.tensor_tensor(L.cw[:], L.picked[:, :, 0, :], L.picked[:, :, 1, :], ALU.add))
                yield
                if not L.first:
                    dve.wait_ge(L.res_stored.sem, L.res_stored.at(0))
                for e in range(E // 2):
                    yield from weigh(L, dve, e)

            def weigh(L, dve, e):
                yield
                dve.wait_ge(L.expert_y.sem, L.expert_y.at(e + 1))
                y = (L.OB, L.M)[e % 2]
                before = L.x if e == 0 else L.res
                for t in range(NT):
                    i = dve.scalar_tensor_tensor(L.res[:, t, :], y[:, t * C:(t + 1) * C], L.cw[:, t, e:e + 1],
                                                 before[:, t, :], ALU.mult, ALU.add)
                i.then_inc(L.acc_done.sem, 1)
                dve.wait_ge(L.acc_done.sem, L.acc_done.at(e + 1))

            def dve_tail(L, dve):
                for e in range(E // 2, E):
                    yield from weigh(L, dve, e)
                dve.tensor_copy(L.diff[:], L.tanh[:]).then_inc(L.res_ready.sem, 1)
                yield
                yield
                yield

            def pe_gate(L, pe):
                for _ in range(4):
                    yield
                pe.wait_ge(L.tok_ready.sem, L.tok_ready.at(1))
                for t in range(NT):
                    i = pe.transpose(L.M[:, t * P:(t + 1) * P], L.tok[:, t, :], ident[:])
                i.then_inc(L.transposed.sem, 1)
                yield
                yield
                pe.wait_ge(L.src_ready.sem, L.src_ready.at(1))
                for t in range(NT):
                    i = pe.matmul(L.OB[:, t * E:(t + 1) * E], L.hT[:, t * P:(t + 1) * P], gw[:], start=True, stop=True)
                i.then_inc(L.gate_ready.sem, 1)
                yield
                yield
                yield

            def act_gate(L, act):
                for _ in range(5):
                    yield
                act.wait_ge(L.transposed.sem, L.transposed.at(1))
                act.activation(L.hT[:], L.M[:, 0:T], ACT.Identity, bias=lnb[:], scale=lnw[:]).then_inc(L.src_ready.sem, 1)
                yield
                yield
                yield
                act.wait_ge(L.gate_diff.sem, L.gate_diff.at(1))
                act.activation(L.tanh[:], L.diff[:], ACT.Tanh, scale=0.5).then_inc(L.gate_w.sem, 1)
                yield

            def pe_start(L, pe, e):
                if e == 0:
                    pe.wait_ge(L.gate_w.sem, L.gate_w.at(1))

            gens = {}

            def pe_head(L, pe):
                yield from pe_gate(L, pe)
                gens[L] = pe_experts(L, pe, E, lambda e, c: w1[:, e, c * P:(c + 1) * P], lambda e, c: w2[:, e, c, :],
                                     lambda e: b2rows[:, e * C:(e + 1) * C], lambda e: pe_start(L, pe, e))
                yield from gens[L]

            def pe_tail(L, pe):
                for _ in range(2):
                    yield

            def act_head(L, act):
                yield from act_gate(L, act)
                yield from act_experts(L, act, E, lambda e, c: b1[:, e, c:c + 1])

            def dve_all(L, dve):
                yield from dve_head(L, dve)
                yield from dve_tail(L, dve)

            def sp_all(L, sp):
                lane = lanes.index(L)
                sp.dma_start(L.x[:], scratch(scratch_a, lane, L.p)).then_inc(L.loaded.sem, 16)
                for _ in range(10 + 10):
                    yield
                sp.wait_ge(L.res_ready.sem, L.res_ready.at(1))
                sp.dma_start(scratch(scratch_b, lane, L.p), L.res[:]).then_inc(L.res_stored.sem, 16)
                yield

            def pool_all(L, pool):
                yield
                yield
                yield from pool_layer_norm(L, pool, 0)
                for _ in range(16):
                    yield

            def none(L, eng):
                yield
                yield

            with nc.Block() as block:
                @block.sync
                def _(sp):
                    run(sp, sp_all, none, "sp")
                    for L in lanes:
                        sp.wait_ge(L.res_stored.sem, L.res_stored.at(16))

                @block.tensor
                def _(pe):
                    run(pe, pe_head, none, "pe")

                @block.scalar
                def _(act):
                    run(act, act_head, none, "act")

                @block.vector
                def _(dve):
                    run(dve, dve_all, none, "dve")

                @block.gpsimd
                def _(pool):
                    run(pool, pool_all, none, "pool")

        phase = ExitStack()
        with phase:
            swap_ctx(phase, "p3")
            lane_common_buffers()
            lane_attention_buffers(False)
            for L in lanes:
                L.resid = L.x

            def pt(name, shape, dtype=F32):
                return phase.enter_context(nc.sbuf_tensor(name, shape, dtype))

            w = {}
            pairs, splits = [], []
            for n in ("l1_wq", "l1_wk", "l1_wv", "l1_wo"):
                w[n] = pt(n, [P, C])
            for n in ("l1_bq", "l1_bk", "l1_ln1_w", "l1_ln1_b"):
                w[n] = pt(n, [P, 1])
            for n in w:
                pairs.append((w[n][:], ins[n]))
            for n in ("l1_bv", "l1_bo"):
                w[n + "2"], raw, low = row(n, C, phase)
                pairs.append((raw[:], ins[n]))
                splits.append((w[n + "2"], raw, low))
            pool_part, dve_part = init_stacks(False)
            load_block(pairs, splits, pool_part, dve_part)
            setup_count["pool"] += 3
            setup_count["dve"] += 2
            F1 = Unit("ffn", 0, 0, 0, 0, wq=w["l1_wq"], wk=w["l1_wk"], wv=w["l1_wv"], wo=w["l1_wo"],
                      bq=w["l1_bq"], bk=w["l1_bk"], bv2=w["l1_bv2"], bo2=w["l1_bo2"], ln_w=w["l1_ln1_w"],
                      ln_b=w["l1_ln1_b"], stack_before=0)
            per = attention_per_unit | project_per
            per |= dict(scores_ready=N_SELF, max_taken=N_SELF, st_ready=N_SELF, exp_done=N_SELF, masked=N_SELF,
                        pv_done=2, o_taken=2, loaded=16, ln_var=1, ln_rstd=1, dve_step=7)
            for L in lanes:
                L.begin_phase(per)

            def dve_head(L, dve):
                for _ in range(3):
                    yield
                dve.wait_ge(L.loaded.sem, L.loaded.at(16))
                yield from dve_layer_norm(L, dve, L.x, 0, 1e-5, L.tok)
                dve.tensor_copy(L.vareps[:], L.rstd[:]).then_inc(L.tok_ready.sem, 1)
                yield
                yield from dve_scores(L, dve, F1)

            def dve_tail(L, dve):
                yield from dve_values(L, dve, F1)
                yield from dve_project(L, dve, F1)
                yield
                yield

            def other_head(scores, norm):
                def head(L, eng):
                    for _ in range(3):
                        yield
                    yield from norm(L, eng, 0)
                    yield
                    yield from scores(L, eng, F1)
                return head

            def other_tail(values, project):
                def tail(L, eng):
                    yield from values(L, eng, F1)
                    if project:
                        yield from project(L, eng, F1)
                    else:
                        for _ in range(4):
                            yield
                    yield
                    yield
                return tail

            def sp_head(L, sp):
                sp.dma_start(L.x[:], scratch(scratch_b, lanes.index(L), L.p)).then_inc(L.loaded.sem, 16)
                for _ in range(6):
                    yield
                yield from sp_scores(L, sp, F1)

            def sp_tail(L, sp):
                yield from sp_values(L, sp, F1)
                for _ in range(4):
                    yield
                sp.wait_ge(L.res_ready.sem, L.res_ready.at(1))
                sp.dma_start(scratch(scratch_a, lanes.index(L), L.p), L.res[:]).then_inc(L.res_stored.sem, 16)
                yield
                yield

            with nc.Block() as block:
                @block.sync
                def _(sp):
                    run(sp, sp_head, sp_tail, "sp")
                    for L in lanes:
                        sp.wait_ge(L.res_stored.sem, L.res_stored.at(16))

                @block.tensor
                def _(pe):
                    run(pe, other_head(pe_scores, idle_norm), other_tail(pe_values, pe_project), "pe")

                @block.scalar
                def _(act):
                    run(act, other_head(act_scores, idle_norm), other_tail(act_values, act_project), "act")

                @block.vector
                def _(dve):
                    run(dve, dve_head, dve_tail, "dve")

                @block.gpsimd
                def _(pool):
                    run(pool, other_head(pool_scores, pool_layer_norm), other_tail(pool_values, None), "pool")

        phase = ExitStack()
        with phase:
            swap_ctx(phase, "p4")
            lane_common_buffers()
            for L in lanes:
                L.hT = L.sb("hT", [P, T])
                L.hsum = L.sb("hsum", [P, 1])
                L.g = L.sb("g", [P, 2, FC, T])
                L.x2 = L.sb("x2", [P, NT, C])
                L.w1 = L.sb("w1", [P, K2, FF])
                L.w2 = L.sb("w2", [P, K2, FC, C])
                L.b1 = L.sb("b1", [P, K2, FC])
                L.b2 = L.sb("b2", [P, K2, C])
                L.logits = L.sb("logits", [1, E])
                L.top = L.sb("top", [1, E])
                L.index = L.sb("index", [1, E], U32)
                L.diff = L.sb("diff", [1, 1])
                L.tanh = L.sb("tanh", [1, 1])
                L.gate2 = L.sb("gate2", [1, K2])
                L.cw = L.sb("cw", [P, K2])
                L.y = L.sb("y", [P, NT, C])
                L.sum = L.sb("sum", [P, NT, C])

            def pt(name, shape, dtype=F32):
                return phase.enter_context(nc.sbuf_tensor(name, shape, dtype))

            gw = pt("m1_gw", [P, E])
            gb = pt("m1_gb", [1, E])
            lnw = pt("m1_lnw", [P, 1])
            lnb = pt("m1_lnb", [P, 1])
            ones_row = pt("ones_row", [1, P])

            def ones(pool, base):
                pool.memset(ones_row[:], 1.0).then_inc(sem_setup_pool, 1)
                pool.wait_ge(sem_setup_pool, base["pool"] + 1)
            load_block([(gw[:], ins["m1_gw"]), (gb[:], ins["m1_gb"]), (lnw[:], ins["m1_lnw"]), (lnb[:], ins["m1_lnb"])],
                       [], ones)
            setup_count["pool"] += 1
            for L in lanes:
                L.begin_phase(moe_per | dict(loaded=32, ln_var=2, ln_rstd=2, gate_diff=1, gate_w=1, gate_row=1,
                                             gate_bcast=1, hidden_ready=2 * K2, gelu_done=2 * K2, expert_y=K2,
                                             acc_done=K2, expert_chosen=1, expert_loaded=16 * 4 * K2, dve_step=14))

            def dve_all(L, dve):
                yield
                yield
                dve.wait_ge(L.loaded.sem, L.loaded.at(32))
                yield from dve_layer_norm(L, dve, L.x, 0, 1e-5, L.tok)
                dve.tensor_copy(L.vareps[:], L.rstd[:]).then_inc(L.tok_ready.sem, 1)
                yield
                yield
                yield
                dve.wait_ge(L.gate_ready.sem, L.gate_ready.at(1))
                link(L, dve, dve.scalar_tensor_tensor(L.logits[:], L.OB[0:1, 0:E], 1.0 / T, gb[:], ALU.mult, ALU.add), apart=True)
                link(L, dve, dve.max(L.top[:], L.logits[:]))
                dve.tensor_tensor(L.diff[:], L.top[:, 0:1], L.top[:, 1:2], ALU.subtract).then_inc(L.gate_diff.sem, 1)
                dve.max_index(L.index[:], L.top[:], L.logits[:]).then_inc(L.expert_chosen.sem, 1)
                yield
                yield
                dve.wait_ge(L.gate_w.sem, L.gate_w.at(1))
                dve.tensor_scalar(L.gate2[:, 0:1], L.tanh[:], 0.5, 0.5, ALU.mult, ALU.add)
                dve.tensor_scalar(L.gate2[:, 1:2], L.tanh[:], -0.5, 0.5, ALU.mult, ALU.add).then_inc(L.gate_row.sem, 1)
                yield
                dve.wait_ge(L.gate_bcast.sem, L.gate_bcast.at(1))
                link(L, dve, dve.tensor_copy(L.cw[:], L.OB[:, 0:K2]))
                for e in range(K2):
                    yield
                    yield
                    dve.wait_ge(L.expert_y.sem, L.expert_y.at(e + 1))
                    y = (L.M, L.R[1])[e]
                    dve.wait_ge(L.expert_loaded.sem, L.expert_loaded.at(16 * 4 * K2))
                    link(L, dve, dve.tensor_tensor(L.y[:], y[:, 0:NT * C].rearrange("p (t c) -> p t c", t=NT),
                                                   L.b2[:, e, None, :].to_broadcast([P, NT, C]), ALU.add))
                    before = L.x if e == 0 else L.sum
                    link(L, dve, dve.scalar_tensor_tensor(L.sum[:].rearrange("p t c -> p (t c)"),
                                                          L.y[:].rearrange("p t c -> p (t c)"), L.cw[:, e:e + 1],
                                                          before[:].rearrange("p t c -> p (t c)"), ALU.mult, ALU.add))
                link(L, dve, dve.tensor_tensor(L.sum[:], L.sum[:], L.x2[:], ALU.add))
                if not L.first:
                    dve.wait_ge(L.res_stored.sem, L.res_stored.at(0))
                yield from dve_layer_norm(L, dve, L.sum, 1, 1e-5, L.res)
                dve.tensor_copy(L.vareps[:], L.rstd[:]).then_inc(L.res_ready.sem, 1)
                yield

            def pe_all(L, pe):
                for _ in range(4):
                    yield
                pe.wait_ge(L.tok_ready.sem, L.tok_ready.at(1))
                for t in range(NT):
                    i = pe.transpose(L.M[:, t * P:(t + 1) * P], L.tok[:, t, :], ident[:])
                i.then_inc(L.transposed.sem, 1)
                yield
                yield
                pe.wait_ge(L.src_ready.sem, L.src_ready.at(1))
                pe.matmul(L.OB[0:1, 0:E], L.hsum[:], gw[:], start=True, stop=True).then_inc(L.gate_ready.sem, 1)
                yield
                yield
                yield
                pe.wait_ge(L.gate_row.sem, L.gate_row.at(1))
                pe.matmul(L.OB[:, 0:K2], ones_row[:], L.gate2[:], start=True, stop=True).then_inc(L.gate_bcast.sem, 1)
                pe.wait_ge(L.expert_loaded.sem, L.expert_loaded.at(16 * 4 * K2))

                def outputs(e):
                    pe.wait_ge(L.gelu_done.sem, L.gelu_done.at(2 * (e + 1)))
                    y = (L.M, L.R[1])[e]
                    for t in range(NT):
                        for c in range(FC):
                            i = pe.matmul(y[:, t * C:(t + 1) * C], L.g[:, e, c, t * P:(t + 1) * P], L.w2[:, e, c, :],
                                          start=(c == 0), stop=(c == FC - 1))
                    i.then_inc(L.expert_y.sem, 1)

                for e in range(K2):
                    for half in range(2):
                        if e >= 1:
                            pe.wait_ge(L.gelu_done.sem, L.gelu_done.at(2 * e - 1 + half))
                        for k in range(2):
                            c = 2 * half + k
                            i = pe.matmul(L.R[half][:, k * T:(k + 1) * T], L.w1[:, e, c * P:(c + 1) * P], L.hT[:],
                                          start=True, stop=True)
                        i.then_inc(L.hidden_ready.sem, 1)
                    yield
                    if e >= 1:
                        outputs(e - 1)
                    yield
                outputs(1)
                yield
                yield
                yield
                yield

            def act_all(L, act):
                for _ in range(5):
                    yield
                act.wait_ge(L.transposed.sem, L.transposed.at(1))
                act.activation(L.hT[:], L.M[:, 0:T], ACT.Identity, bias=lnb[:], scale=lnw[:],
                               accum_out=L.hsum[:]).then_inc(L.src_ready.sem, 1)
                yield
                yield
                yield
                act.wait_ge(L.gate_diff.sem, L.gate_diff.at(1))
                act.activation(L.tanh[:], L.diff[:], ACT.Tanh, scale=0.5).then_inc(L.gate_w.sem, 1)
                yield
                for e in range(K2):
                    for half in range(2):
                        act.wait_ge(L.hidden_ready.sem, L.hidden_ready.at(2 * e + half + 1))
                        for k in range(2):
                            c = 2 * half + k
                            i = act.activation(L.g[:, e, c, :], L.R[half][:, k * T:(k + 1) * T], ACT.Gelu,
                                               bias=L.b1[:, e, c:c + 1])
                        i.then_inc(L.gelu_done.sem, 1)
                    yield
                    yield
                for _ in range(4):
                    yield

            def sp_all(L, sp):
                lane = lanes.index(L)
                sp.dma_start(L.x[:], scratch(scratch_a, lane, L.p)).then_inc(L.loaded.sem, 16)
                sp.dma_start(L.x2[:], scratch(scratch_x2, lane, L.p)).then_inc(L.loaded.sem, 16)
                for _ in range(8):
                    yield
                sp.wait_ge(L.expert_chosen.sem, L.expert_chosen.at(1))
                sp.sem_inc(held_sp, 1)
                for k in range(K2):
                    e = sp.value_load(L.index[0:1, k:k + 1], min_val=0, max_val=E - 1)
                    one = lambda d, s: d[bass.ds(e, 1)].rearrange(s)
                    sp.dma_start(L.w1[:, k, :], one(ins["m1_w1"], "o p f -> p (o f)")).then_inc(L.expert_loaded.sem, 16)
                    sp.dma_start(L.w2[:, k], one(ins["m1_w2"], "o p c n -> p (o c) n")).then_inc(L.expert_loaded.sem, 16)
                    sp.dma_start(L.b1[:, k], one(ins["m1_b1"], "o p c -> p (o c)")).then_inc(L.expert_loaded.sem, 16)
                    sp.dma_start(L.b2[:, k], ins["m1_b2"][bass.ds(e, 1)].to_broadcast([P, C])).then_inc(
                        L.expert_loaded.sem, 16)
                for _ in range(9):
                    yield
                sp.wait_ge(L.res_ready.sem, L.res_ready.at(1))
                sp.dma_start(token_major(out, lane, L.p), L.res[:]).then_inc(L.res_stored.sem, 16)
                yield

            def pool_all(L, pool):
                yield
                yield
                yield from pool_layer_norm(L, pool, 0)
                for _ in range(10):
                    yield
                yield from pool_layer_norm(L, pool, 1)
                yield

            def none(L, eng):
                yield
                yield

            with nc.Block() as block:
                @block.sync
                def _(sp):
                    run(sp, sp_all, none, "sp")
                    for L in lanes:
                        sp.wait_ge(L.res_stored.sem, L.res_stored.at(16))

                @block.tensor
                def _(pe):
                    run(pe, pe_all, none, "pe")

                @block.scalar
                def _(act):
                    run(act, act_all, none, "act")

                @block.vector
                def _(dve):
                    run(dve, dve_all, none, "dve")

                @block.gpsimd
                def _(pool):
                    run(pool, pool_all, none, "pool")



def _by_lane(a):
    return a.reshape(a.shape[:-1] + (S4, S4, DH)).swapaxes(-3, -2).swapaxes(-2, -1).reshape(a.shape)


def _layout(i):
    d = {"x": i["x"], "ctxT": i["ctx_768"].transpose(0, 2, 1),
         "pad": i["mask_BxS_bk0"].reshape(B, NT, P).transpose(0, 2, 1)}
    d["a_wq"], d["a_wk"], d["a_wv"] = _by_lane(i["L0_attn_Wq"]), _by_lane(i["L0_attn_Wk"]), i["L0_attn_Wv"]
    d["a_bq"] = _by_lane(i["L0_attn_bq"]).reshape(C, 1)
    d["a_bk"] = _by_lane(i["L0_attn_bk"]).reshape(1, C)
    d["a_bv"] = i["L0_attn_bv"].reshape(1, C)
    d["a_gamma"] = i["L0_attn_gamma"].reshape(1, C)
    d["a_beta"] = i["L0_attn_beta"].reshape(1, C)
    d["x_wq"] = _by_lane(i["L0_xattn_Wq"].T)
    d["x_wk"] = _by_lane(i["L0_xattn_Wkv"][:C].T)
    d["x_wv"] = i["L0_xattn_Wkv"][C:].T
    for n in range(2):
        f = lambda k: i["L0_ffn_" + k][n]
        d[f"l{n}_wq"], d[f"l{n}_wk"] = _by_lane(f("wq")), _by_lane(f("wk"))
        d[f"l{n}_wv"], d[f"l{n}_wo"] = f("wv"), f("wo")
        d[f"l{n}_bq"], d[f"l{n}_bk"] = _by_lane(f("bq")).reshape(C, 1), _by_lane(f("bk")).reshape(C, 1)
        d[f"l{n}_bv"], d[f"l{n}_bo"] = f("bv").reshape(1, C), f("bo").reshape(1, C)
        d[f"l{n}_ln1_w"], d[f"l{n}_ln1_b"] = f("ln1_w").reshape(C, 1), f("ln1_b").reshape(C, 1)
        d[f"m{n}_lnw"], d[f"m{n}_lnb"] = f("ln2_w").reshape(C, 1), f("ln2_b").reshape(C, 1)
        d[f"m{n}_gw"], d[f"m{n}_gb"] = f("gate_w"), f("gate_b").reshape(1, E)
        d[f"m{n}_w1"] = f("e_w1")
        d[f"m{n}_w2"] = f("e_w2").reshape(E, FC, P, C).transpose(0, 2, 1, 3)
        b1 = f("e_b1").reshape(E, FC, P)
        d[f"m{n}_b1"] = b1.transpose(2, 0, 1) if n == 0 else b1.transpose(0, 2, 1)
        d[f"m{n}_b2"] = f("e_b2").reshape(1, E * C) if n == 0 else f("e_b2")
    return {k: np.ascontiguousarray(v) for k, v in d.items()}


def kernel(**inputs):
    import concourse.bacc as _bacc
    from concourse.bass_utils import run_bass_kernel_spmd as _run

    arrays = _layout({k: np.asarray(v) for k, v in inputs.items()})
    nc = _bacc.Bacc("TRN2", target_bir_lowering=False, num_devices=1)
    ins = {k: nc.dram_tensor(f"in_{k}", a.shape, mybir.dt.from_np(a.dtype), kind="ExternalInput").ap()
           for k, a in arrays.items()}
    out = nc.dram_tensor("out", (B, T, C), F32, kind="ExternalOutput").ap()
    decoder(nc, ins, out)
    r = _run(nc, [{f"in_{k}": a for k, a in arrays.items()}], core_ids=[0])
    return r.results[0]["out"]
```

```python
from contextlib import ExitStack

import numpy as np

import concourse.bass as bass
from concourse import mybir

ALU = mybir.AluOpType
ACT = mybir.ActivationFunctionType
AX = mybir.AxisListType
F32 = mybir.dt.float32
F32R = mybir.dt.float32r
BF16 = mybir.dt.bfloat16
U8 = mybir.dt.uint8
U32 = mybir.dt.uint32

P = 128
B = 16
T = 256
NT = T // P
C = 128
H = 16
DH = C // H
S4 = 4
TC = 64
CC = 96
E = 8
FF = 512
FC = FF // P
K2 = 2
BIAS_ROWS = (("a_bk", C), ("a_bv", C), ("l0_bv", C), ("l0_bo", C), ("l1_bv", C), ("l1_bo", C), ("m0_b2", E * C))
MROW = 3 * 32
MREND = MROW + 8
PASSES = B // 2
SCALE = float(DH) ** -0.5
BIG = float(2 ** 32)
HIDE = -1.0e30


class AT:
    src_taken = 0
    qk, v = 3, 4
    qk_taken, v_taken = 3, 4
    split = 5
    spread = (5, 6, 7, 9)
    keys = (5, 9)
    queries = (8, 10)
    rounds = 10
    maxima, maxima_taken = 1, 1
    end = 1
    values = 3
    tick_after_scores = (1, 5, 7, 9)
    tick_after_values = (0, 1, 2, 3, 4, 5, 6, 7, 8, 9, 10, 11)


class Signal:

    def __init__(self, sem, lane):
        self.sem, self.lane, self.base, self.per = sem, lane, 0, 0

    def begin(self, per):
        self.base += PASSES * self.per
        self.per = per

    def at(self, n):
        return self.lane.p * self.per + (self.base + n)


class Lane:

    def __init__(self, name, ctx, nc):
        self.name, self.ctx, self.nc = name, ctx, nc
        self.p = 0
        self.sig = {}
        self.loaded = self.counted("loaded")
        self.tok_ready = self.counted("tok_ready")
        self.transposed = self.counted("transposed")
        self.src_ready = self.counted("src_ready")
        self.projected = self.counted("projected")
        self.qk_taken = self.counted("qk_taken")
        self.v_taken = self.counted("v_taken")
        self.split_ready = self.counted("split_ready")
        self.spread_ready = self.counted("spread_ready")
        self.stack_by_act = self.counted("stack_by_act")
        self.stack_by_dve = self.counted("stack_by_dve")
        self.scores_ready = self.counted("scores_ready")
        self.max_taken = self.counted("max_taken")
        self.maxparts_ready = self.counted("maxparts_ready")
        self.maxT_ready = self.counted("maxT_ready")
        self.maxrows_by_act = self.counted("maxrows_by_act")
        self.maxrows_by_dve = self.counted("maxrows_by_dve")
        self.st_ready = self.counted("st_ready")
        self.exp_done = self.counted("exp_done")
        self.masked = self.counted("masked")
        self.pv_done = self.counted("pv_done")
        self.o_taken = self.counted("o_taken")
        self.oT_ready = self.counted("oT_ready")
        self.ao_ready = self.counted("ao_ready")
        self.aoT_ready = self.counted("aoT_ready")
        self.aoT_taken = self.counted("aoT_taken")
        self.y_ready = self.counted("y_ready")
        self.x2_ready = self.counted("x2_ready")
        self.x2_stored = self.counted("x2_stored")
        self.resid_ready = self.counted("resid_ready")
        self.res_ready = self.counted("res_ready")
        self.res_stored = self.counted("res_stored")
        self.ln_var = self.counted("ln_var")
        self.ln_rstd = self.counted("ln_rstd")
        self.dve_step = self.counted("dve_step")
        self.gate_ready = self.counted("gate_ready")
        self.gate_diff = self.counted("gate_diff")
        self.gate_w = self.counted("gate_w")
        self.hidden_ready = self.counted("hidden_ready")
        self.gelu_done = self.counted("gelu_done")
        self.expert_y = self.counted("expert_y")
        self.acc_done = self.counted("acc_done")
        self.expert_chosen = self.counted("expert_chosen")
        self.expert_loaded = self.counted("expert_loaded")
        self.gate_row = self.counted("gate_row")
        self.sums_ready = self.counted("sums_ready")
        self.gate_bcast = self.counted("gate_bcast")
        self.dve_steps = 0

    def counted(self, name):
        signal = Signal(self.ctx.enter_context(self.nc.semaphore(f"{self.name}_{name}")), self)
        self.sig[name] = signal
        return signal

    def begin_phase(self, per):
        for s, signal in self.sig.items():
            signal.begin(per.get(s, 0))

    def sb(self, name, shape, dtype=F32):
        return self.ctx.enter_context(self.nc.sbuf_tensor(f"{self.name}_{name}", shape, dtype))


SELF_ROUNDS = [(0, s, None) for s in range(S4)] + [(1, s, u) for s in range(S4) for u in range(2)]
N_SELF = len(SELF_ROUNDS)
N_CTX = 4
SPREAD = (1, 1, 0, 0, 1, 0, 1)
QUERY_PARTS = (0, 2)
KEY_PARTS = (4, 3)


class Unit:

    def __init__(self, kind, index, rounds_before, pv_before, masks_before, wq, wk, wv,
                 wo=None, bq=None, bk=None, bk2=None, bv2=None, bo2=None, ln_w=None, ln_b=None):
        self.kind, self.u = kind, index
        self.rounds = N_CTX if kind == "ctx" else N_SELF
        self.before, self.pv_before, self.masks_before = rounds_before, pv_before, masks_before
        self.wq, self.wk, self.wv, self.wo = wq, wk, wv, wo
        self.bq, self.bk, self.bk2, self.bv2, self.bo2 = bq, bk, bk2, bv2, bo2
        self.ln_w, self.ln_b = ln_w, ln_b


def decoder(nc, ins, out):
    top = ExitStack()
    with top:
        sem_setup_dma = top.enter_context(nc.semaphore("setup_loaded"))
        sem_late_dma = top.enter_context(nc.semaphore("late_weights_loaded"))
        sem_w1_hi = top.enter_context(nc.semaphore("w1_hi_ready"))
        sem_setup = top.enter_context(nc.semaphore("setup_step"))
        sem_setup_pool = top.enter_context(nc.semaphore("setup_pool_step"))
        lanes = [Lane(n, top, nc) for n in ("even", "odd")]
        held_dve, held_pool, held_sp = (top.enter_context(nc.semaphore(f"held_{e}")) for e in ("dve", "pool", "sp"))

        for L in lanes:
            def bank(n):
                return top.enter_context(nc.psum_tensor(f"{L.name}_{n}", [P, 512], F32))
            L.R = [bank("round0"), bank("round1")]
            L.OB = bank("values")
            L.M = bank("mixed")
            L.S = L.R + [L.M, L.OB]
            L.ST = L.R + [L.M]

        def const(name, shape, dtype=F32):
            return top.enter_context(nc.sbuf_tensor(name, shape, dtype))

        ident = const("ident", [P, P])
        ones2 = const("ones2", [2, P], F32R)
        scratch_x2 = [nc.dram_tensor(f"scratch_x2_{n}", [PASSES, P, NT, C], F32).ap() for n in range(2)]
        scratch_a = [nc.dram_tensor(f"scratch_a_{n}", [PASSES, P, NT, C], F32).ap() for n in range(2)]
        scratch_b = [nc.dram_tensor(f"scratch_b_{n}", [PASSES, P, NT, C], F32).ap() for n in range(2)]

        def token_major(dram, lane, p):
            pairs = dram.rearrange("(p l) (n t) c -> l p t n c", l=2, t=P)
            return pairs[lane][bass.ds(p, 1)].rearrange("o t n c -> t (o n) c")

        def scratch(drams, lane, p):
            return drams[lane][bass.ds(p, 1)].rearrange("o t n c -> t (o n) c")


        def link(L, dve, instruction, apart=False):
            L.dve_steps += 1
            instruction.then_inc(L.dve_step.sem, 1)
            if apart:
                dve.wait_ge(L.dve_step.sem, L.dve_step.at(L.dve_steps))
                dve.sem_inc(held_dve, 1)
            else:
                dve.wait_ge(L.dve_step.sem, L.dve_step.at(L.dve_steps))

        def dve_layer_norm(L, dve, z, n, normed, weight=None, offset=None, ready=None, eps=1e-5):
            for t in range(NT):
                i = dve.bn_stats(L.stats[:, t, :], z[:, t, :])
            link(L, dve, i, apart=True)
            for t in range(NT):
                i = dve.bn_aggr(L.meanvar[:, t, :], L.stats[:, t, :])
            link(L, dve, i)
            dve.tensor_scalar(L.vareps[:], L.meanvar[:, :, 1], eps, None, ALU.add).then_inc(L.ln_var.sem, 1)
            if weight is not None:
                for t in range(NT):
                    i = dve.scalar_tensor_tensor(normed[:, t, :], z[:, t, :], L.meanvar[:, t, 0:1], weight[:],
                                                 ALU.subtract, ALU.mult)
                link(L, dve, i)
            yield
            yield
            dve.wait_ge(L.ln_rstd.sem, L.ln_rstd.at(n + 1))
            for t in range(NT):
                if weight is None:
                    i = dve.tensor_scalar(normed[:, t, :], z[:, t, :], L.meanvar[:, t, 0:1], L.rstd[:, t:t + 1],
                                          ALU.subtract, ALU.mult)
                else:
                    i = dve.scalar_tensor_tensor(normed[:, t, :], normed[:, t, :], L.rstd[:, t:t + 1],
                                                 offset[:, t, :], ALU.mult, ALU.add)
            if ready is None:
                link(L, dve, i)
            else:
                i.then_inc(ready.sem, 1)

        def pool_layer_norm(L, pool, n):
            yield
            pool.wait_ge(L.ln_var.sem, L.ln_var.at(n + 1))
            pool.tensor_tensor(L.rstd[:], L.vareps[:], minus_half[:], ALU.pow).then_inc(L.ln_rstd.sem, 1)
            yield



        def pause(now, then):
            for _ in range(then - now):
                yield

        def between_scores(U, r):
            if U.kind == "ctx" or r in AT.tick_after_scores:
                yield

        def between_values(U, r):
            if U.kind == "ctx" or r in AT.tick_after_values:
                yield

        def pe_scores(L, pe, U):
            u = U.u
            pe.wait_ge(L.tok_ready.sem, L.tok_ready.at(u + 1))
            for t in range(NT):
                i = pe.transpose(L.M[:, t * P:(t + 1) * P], L.tok[:, t, :], ident[:])
            if U.kind == "self":
                for t in range(NT):
                    i = pe.transpose(L.M[0:2, T + t * P:T + (t + 1) * P], L.keep2[:, t, :], ident[:])
            i.then_inc(L.transposed.sem, 1)
            yield from pause(0, AT.qk)
            pe.wait_ge(L.src_ready.sem, L.src_ready.at(u + 1))
            pe.matmul(L.M[:, 0:T], U.wq[:], L.srcT[:], start=True, stop=True)
            if U.kind == "ctx":
                i = pe.matmul(L.M[:, T:T + TC], U.wk[:], L.ctxT[:, 0:TC], start=True, stop=True)
            else:
                i = pe.matmul(L.M[:, T:2 * T], U.wk[:], L.srcT[:], start=True, stop=U.kind != "self")
                if U.kind == "self":
                    i = pe.matmul(L.M[:, T:2 * T], U.bk2[:], L.keeprows[:], start=False, stop=True)
            i.then_inc(L.projected.sem, 1)
            yield from pause(AT.qk, AT.v)
            if U.kind == "ctx":
                i = pe.matmul(L.OB[:, 0:C], L.ctxT[:], U.wv[:], start=True, stop=True)
            else:
                for t in range(NT):
                    cols = slice(t * C, (t + 1) * C)
                    pe.matmul(L.OB[:, cols], L.srcT[:, t * P:(t + 1) * P], U.wv[:], start=True, stop=False)
                    i = pe.matmul(L.OB[:, cols], ones2[:], U.bv2[:], start=False, stop=True)
            i.then_inc(L.projected.sem, 1)
            yield from pause(AT.v, AT.spread[0])
            pe.wait_ge(L.split_ready.sem, L.split_ready.at(u + 1))
            nk = TC if U.kind == "ctx" else T
            done = 0
            for part in range(2):
                keys, queries = ((L.R[1], L.R[0]), (L.M, L.OB))[part]
                for to, n, first, parts in ((keys, nk, T, KEY_PARTS), (queries, T, 0, QUERY_PARTS)):
                    if to is L.OB:
                        pe.wait_ge(L.v_taken.sem, L.v_taken.at(u + 1))
                    for j in range(2):
                        for src, window in zip((L.HI, L.LO), parts):
                            i = pe.matmul(to[0:MROW, j * n:(j + 1) * n],
                                          spread[:, 2 * part + j, 32 * window:32 * window + MROW],
                                          src[:, first:first + n], start=src is L.HI, stop=src is L.LO)
                    i.then_inc(L.spread_ready.sem, 1)
                    done += 1
                    yield from pause(AT.spread[done - 1], AT.spread[done] if done < 4 else AT.rounds)
            for r in range(U.rounds):
                if r == 0:
                    pe.wait_ge(L.stack_by_act.sem, L.stack_by_act.at(2 * u + 1))
                    pe.wait_ge(L.stack_by_dve.sem, L.stack_by_dve.at(2 * u + 1))
                if r == (1 if U.kind == "ctx" else 2):
                    pe.wait_ge(L.stack_by_act.sem, L.stack_by_act.at(2 * u + 2))
                    pe.wait_ge(L.stack_by_dve.sem, L.stack_by_dve.at(2 * u + 2))
                if r >= len(L.S):
                    pe.wait_ge(L.max_taken.sem, L.max_taken.at(U.before + r - len(L.S) + 1))
                bank = L.S[r % len(L.S)]
                if U.kind == "ctx":
                    t = r // 2
                    for k in range(2):
                        s = 2 * (r % 2) + k
                        i = pe.matmul(bank[:, k * 256:(k + 1) * 256], L.Q[0:MROW, s, t * P:(t + 1) * P],
                                      L.KX[0:MROW, s].rearrange("p a k -> p (a k)"),
                                      start=True, stop=True)
                else:
                    t, s, half = SELF_ROUNDS[r]
                    if t == 0:
                        pe.matmul(bank[:], L.Q[0:MROW, s, 0:P], L.K[0:MROW, 4 * s:4 * s + 4, 0:P],
                                  start=True, stop=False)
                        i = pe.matmul(bank[:], ident_bf[:], hide[:, None, :].to_broadcast([P, 4, P]),
                                      start=False, stop=True)
                    else:
                        pe.matmul(bank[:], L.Q[0:MROW, s, P:T], L.K[0:MROW, 4 * s + 2 * half:4 * s + 2 * half + 2, :],
                                  start=True, stop=False)
                        i = pe.matmul(bank[:].rearrange("p (h k) -> p h k", h=2)[:, :, P:T], ident_bf[:],
                                      hide[:, None, :].to_broadcast([P, 2, P]), start=False, stop=True)
                i.then_inc(L.scores_ready.sem, 1)
                yield from between_scores(U, r)
            yield from pause(0, AT.maxima)
            pe.wait_ge(L.maxparts_ready.sem, L.maxparts_ready.at(u + 1))
            for s in range(S4):
                for t in range(NT):
                    i = pe.matmul((L.M, L.OB)[s // 2][0:MREND, (s % 2) * T + t * P:(s % 2) * T + (t + 1) * P],
                                  L.maxparts[:, t, s], ident_r[:], start=True, stop=True)
                if s % 2 == 1:
                    i.then_inc(L.maxT_ready.sem, 1)
            yield from pause(AT.maxima, AT.end)

        def act_scores(L, act, U):
            u = U.u
            yield from pause(0, AT.src_taken)
            act.wait_ge(L.transposed.sem, L.transposed.at(u + 1))
            if U.kind == "self":
                act.copy(L.keeprows[:], L.M[0:2, T:2 * T])
            if U.kind == "ffn":
                i = act.activation(L.srcT[:], L.M[:, 0:T], ACT.Identity, bias=U.ln_b[:], scale=U.ln_w[:])
            else:
                i = act.copy(L.srcT[:], L.M[:, 0:T])
            i.then_inc(L.src_ready.sem, 1)
            yield from pause(AT.src_taken, AT.qk_taken)
            act.wait_ge(L.projected.sem, L.projected.at(2 * u + 1))
            func = ACT.Relu if U.kind == "self" else ACT.Identity
            if U.kind == "ctx":
                act.copy(L.QK[:, 0:T], L.M[:, 0:T])
                i = act.copy(L.QK[:, T:T + TC], L.M[:, T:T + TC])
            else:
                act.activation(L.QK[:, 0:T], L.M[:, 0:T], func, bias=U.bq[:])
                if U.kind == "self":
                    i = act.activation(L.QK[:, T:2 * T], L.M[:, T:2 * T], func)
                else:
                    i = act.activation(L.QK[:, T:2 * T], L.M[:, T:2 * T], func, bias=U.bk[:])
            i.then_inc(L.qk_taken.sem, 1)
            yield from pause(AT.qk_taken, AT.v_taken)
            act.wait_ge(L.projected.sem, L.projected.at(2 * u + 2))
            if U.kind == "ctx":
                for k in range(2):
                    rows = slice(k * TC, (k + 1) * TC)
                    i = act.copy(L.VX[rows, :, 16 * k:16 * k + DH],
                                 L.OB[rows, 0:C].rearrange("p (n k d) -> p n k d", k=2, d=DH)[:, :, k, :])
            else:
                i = act.activation(L.V[:, :, :, 0:DH], L.OB[:, 0:NT * C].rearrange("p (n h d) -> p n h d", n=NT, d=DH),
                                   func)
            i.then_inc(L.v_taken.sem, 1)
            yield from pause(AT.v_taken, AT.queries[0])
            act.wait_ge(L.spread_ready.sem, L.spread_ready.at(4 * u + 2))
            act.copy(L.Q[0:MROW, 0:2, :].rearrange("p s q -> p (s q)"), L.R[0][0:MROW, :]).then_inc(L.stack_by_act.sem, 1)
            yield from pause(AT.queries[0], AT.keys[1])
            act.wait_ge(L.spread_ready.sem, L.spread_ready.at(4 * u + 3))
            for a in range(S4):
                i = act.activation(stacked_keys(L, U, 1, a), spread_keys(L, U, 1), ACT.Copy,
                                   scale=own_rows[0:MROW, a:a + 1])
            i.then_inc(L.stack_by_act.sem, 1)
            yield from pause(AT.keys[1], AT.rounds)
            for r in range(U.rounds):
                yield from between_scores(U, r)
            yield from pause(0, AT.maxima_taken)
            act.wait_ge(L.maxT_ready.sem, L.maxT_ready.at(2 * u + 1))
            act.copy(L.Q[MROW:MREND, 0:2, :].rearrange("p s q -> p (s q)"),
                     L.M[MROW:MREND, :]).then_inc(L.maxrows_by_act.sem, 1)
            yield from pause(AT.maxima_taken, AT.end)

        def stacked_keys(L, U, part, a):
            if U.kind == "ctx":
                return L.KX[0:MROW, 2 * part:2 * part + 2, a, :]
            return L.K[0:MROW, 8 * part + a:8 * part + 8:S4, :]

        def spread_keys(L, U, part):
            n = TC if U.kind == "ctx" else T
            return (L.R[1], L.M)[part][0:MROW, 0:2 * n].rearrange("p (s k) -> p s k", s=2)

        def dve_scores(L, dve, U):
            yield from pause(0, AT.split)
            dve.wait_ge(L.qk_taken.sem, L.qk_taken.at(U.u + 1))
            n = T + (TC if U.kind == "ctx" else T)
            link(L, dve, dve.tensor_copy(L.HI[:, 0:n], L.QK[:, 0:n]))
            dve.tensor_tensor(L.LO[:, 0:n], L.QK[:, 0:n], L.HI[:, 0:n].bitcast(F32),
                              ALU.subtract).then_inc(L.split_ready.sem, 1)
            yield from pause(AT.split, AT.keys[0])
            dve.wait_ge(L.spread_ready.sem, L.spread_ready.at(4 * U.u + 1))
            for a in range(S4):
                i = dve.tensor_scalar(stacked_keys(L, U, 0, a), spread_keys(L, U, 0), own_rows[0:MROW, a:a + 1],
                                      None, ALU.mult)
            i.then_inc(L.stack_by_dve.sem, 1)
            yield from pause(AT.keys[0], AT.queries[1])
            dve.wait_ge(L.spread_ready.sem, L.spread_ready.at(4 * U.u + 4))
            dve.tensor_copy(L.Q[0:MROW, 2:4, :].rearrange("p s q -> p (s q)"),
                            L.OB[0:MROW, :]).then_inc(L.stack_by_dve.sem, 1)
            yield from pause(AT.queries[1], AT.rounds)
            for r in range(U.rounds):
                dve.wait_ge(L.scores_ready.sem, L.scores_ready.at(U.before + r + 1))
                bank = L.S[r % len(L.S)]
                if U.kind == "ctx":
                    t, s0 = r // 2, 2 * (r % 2)
                    for k in range(2):
                        i = dve.tensor_reduce(L.negmax[:, t, :, s0 + k],
                                              bank[:, k * 256:(k + 1) * 256].rearrange("p (a k) -> p a k", a=4),
                                              AX.X, ALU.max, negate=True)
                else:
                    t, s, half = SELF_ROUNDS[r]
                    heads = slice(0, 4) if t == 0 else slice(2 * half, 2 * half + 2)
                    i = dve.tensor_reduce(L.negmax[:, t, heads, s],
                                          bank[:].rearrange("p (a k) -> p a k", k=P * (t + 1)),
                                          AX.X, ALU.max, negate=True)
                i.then_inc(L.max_taken.sem, 1)
                yield from between_scores(U, r)
            dve.wait_ge(L.max_taken.sem, L.max_taken.at(U.before + U.rounds))
            negmax = L.negmax[:].rearrange("p t a s -> p t s a")
            high, low = L.maxparts[:, :, :, MROW:MROW + S4], L.maxparts[:, :, :, MROW + S4:MREND]
            link(L, dve, dve.tensor_copy(high, negmax))
            dve.tensor_tensor(low, negmax, high.bitcast(F32), ALU.subtract).then_inc(L.maxparts_ready.sem, 1)
            yield from pause(0, AT.maxima_taken)
            dve.wait_ge(L.maxT_ready.sem, L.maxT_ready.at(2 * U.u + 2))
            dve.tensor_copy(L.Q[MROW:MREND, 2:4, :].rearrange("p s q -> p (s q)"),
                            L.OB[MROW:MREND, :]).then_inc(L.maxrows_by_dve.sem, 1)
            yield from pause(AT.maxima_taken, AT.end)

        def pool_scores(L, pool, U):
            yield from pause(0, AT.rounds)
            for r in range(U.rounds):
                yield from between_scores(U, r)
            yield from pause(0, AT.end)


        def pe_values(L, pe, U):
            yield from pause(0, AT.values)
            u = U.u
            def first_keys(s):
                pe.wait_ge(L.masked.sem, L.masked.at(U.masks_before + 6 * (s // 2) + 2 * (s % 2) + 2))
                if s == 0:
                    pe.wait_ge(L.maxrows_by_dve.sem, L.maxrows_by_dve.at(u + 1))
                if s == 2:
                    pe.wait_ge(L.o_taken.sem, L.o_taken.at(U.pv_before + 1))
                for a in range(S4):
                    r = 6 * (s // 2) + 2 * (s % 2) + a // 2
                    pe.matmul(L.OB[32 * a:32 * a + 32, (s % 2) * T:(s % 2 + 1) * T], L.V[:, 0, 4 * s + a, :],
                              L.probs[:, r, (a % 2) * T:(a % 2 + 1) * T], start=(s % 2 == 0), stop=False,
                              tile_position=(0, 32 * a), skip_group_check=True)

            def second_keys(pair):
                pe.wait_ge(L.masked.sem, L.masked.at(U.masks_before + 6 * pair + 6))
                for s in (2 * pair, 2 * pair + 1):
                    for a in range(S4):
                        i = pe.matmul(L.OB[32 * a:32 * a + 32, (s % 2) * T + P:(s % 2 + 1) * T], L.V[:, 1, 4 * s + a, :],
                                      L.probs[:, 6 * pair + 4 + s % 2, a * P:(a + 1) * P], start=False,
                                      stop=True, tile_position=(0, 32 * a), skip_group_check=True)
                i.then_inc(L.pv_done.sem, 1)

            for r in range(U.rounds):
                if r == 0:
                    pe.wait_ge(L.maxrows_by_act.sem, L.maxrows_by_act.at(u + 1))
                if r == (2 if U.kind == "ctx" else 6):
                    pe.wait_ge(L.maxrows_by_dve.sem, L.maxrows_by_dve.at(u + 1))
                if r >= len(L.ST):
                    pe.wait_ge(L.exp_done.sem, L.exp_done.at(U.before + r - len(L.ST) + 1))
                bank = L.ST[r % len(L.ST)]
                if U.kind == "ctx":
                    for k in range(2):
                        i = pe.matmul(bank[:, k * T:(k + 1) * T], L.KX[0:MREND, r, 2 * k:2 * k + 2, :].rearrange("p a k -> p (a k)"), L.Q[0:MREND, r, :],
                                      start=True, stop=True)
                    i.then_inc(L.st_ready.sem, 1)
                    if r >= 2:
                        context_values(L, pe, U, r - 2)
                else:
                    pair, j = divmod(r, 6)
                    if j < 4:
                        s = 2 * pair + j // 2
                        for k in range(2):
                            i = pe.matmul(bank[:, k * T:(k + 1) * T], L.K[0:MREND, 4 * s + 2 * (j % 2) + k, 0:P],
                                          L.Q[0:MREND, s, :], start=True, stop=True)
                    else:
                        s = 2 * pair + j - 4
                        for a in range(S4):
                            i = pe.matmul(bank[:, a * P:(a + 1) * P], L.K[0:MREND, 4 * s + a, P:T],
                                          L.Q[0:MREND, s, P:T], start=True, stop=True)
                    i.then_inc(L.st_ready.sem, 1)
                    if j == 3:
                        first_keys(2 * pair)
                    if j == 5:
                        first_keys(2 * pair + 1)
                    if r == 7:
                        second_keys(0)
                yield from between_values(U, r)
            if U.kind == "ctx":
                context_values(L, pe, U, 2)
                context_values(L, pe, U, 3)
            else:
                second_keys(1)
            yield
            slots = 2 if U.kind == "ctx" else 4
            pe.wait_ge(L.o_taken.sem, L.o_taken.at(U.pv_before + (1 if U.kind == "ctx" else 2)))
            for t in range(NT):
                to = (L.M, L.R[0])[t]
                for s in range(slots):
                    i = pe.transpose(to[:, s * P:(s + 1) * P],
                                     L.O[:, s // 2, (s % 2) * T + t * P:(s % 2) * T + (t + 1) * P], ident[:])
            i.then_inc(L.oT_ready.sem, 1)
            yield
            yield

        def context_values(L, pe, U, s):
            pe.wait_ge(L.exp_done.sem, L.exp_done.at(U.before + s + 1))
            for k in range(2):
                c = (s % 2) * 2 + k
                i = pe.matmul(L.OB[32 * c:32 * c + 32, (s // 2) * T:(s // 2 + 1) * T], L.VX[:, 2 * s + k, :],
                              L.probs[:, s, k * T:(k + 1) * T], start=True, stop=True, tile_position=(0, 32 * c))
            if s == S4 - 1:
                i.then_inc(L.pv_done.sem, 1)

        def act_values(L, act, U):
            yield from pause(0, AT.values)
            u = U.u
            def take_outputs(half):
                act.wait_ge(L.pv_done.sem, L.pv_done.at(U.pv_before + half + 1))
                act.copy(L.O[:, half, :], L.OB[:]).then_inc(L.o_taken.sem, 1)

            for r in range(U.rounds):
                act.wait_ge(L.st_ready.sem, L.st_ready.at(U.before + r + 1))
                bias = {}
                if U.kind == "self":
                    bias["bias"] = L.keybias[:, 0:1] if r % 6 < 4 else L.keybias[:, 1:2]
                act.activation(L.probs[:, r, :], L.ST[r % len(L.ST)][:], ACT.Exp, scale=SCALE,
                               **bias).then_inc(L.exp_done.sem, 1)
                if U.kind != "ctx" and r == 8:
                    take_outputs(0)
                yield from between_values(U, r)
            take_outputs(0 if U.kind == "ctx" else 1)
            yield
            yield
            yield

        def pool_values(L, pool, U):
            yield from pause(0, AT.values)
            for r in range(U.rounds):
                if U.kind != "ctx":
                    pool.wait_ge(L.exp_done.sem, L.exp_done.at(U.before + r + 1))
                    pool.sem_inc(held_pool, 1)
                    heads, width = (2, T) if r % 6 < 4 else (4, P)
                    block = L.probs[:, r, :].rearrange("p (h q) -> p h q", h=heads)[:, :, 0:P]
                    pool.affine_select(out=block, in_=block, compare_op=ALU.is_ge, fill=0.0, base=0,
                                       pattern=[[0, heads], [1, P]], channel_multiplier=-1).then_inc(L.masked.sem, 1)
                yield from between_values(U, r)
            for _ in range(3):
                yield

        def dve_values(L, dve, U):
            yield from pause(0, AT.values)
            for r in range(U.rounds):
                yield from between_values(U, r)
            yield
            yield
            dve.wait_ge(L.oT_ready.sem, L.oT_ready.at(U.u + 1))
            w = 16 if U.kind == "ctx" else 32
            for t in range(NT):
                o = (L.M, L.R[0])[t][:, 0:H * w].rearrange("p (h r) -> p h r", r=w)
                if U.kind == "self":
                    i = dve.tensor_scalar(L.denom[:, t, :], o[:, :, DH], 1e-30, None, ALU.max)
                else:
                    i = dve.reciprocal(L.denom[:, t, :], o[:, :, DH])
            link(L, dve, i)
            if U.kind == "self":
                link(L, dve, dve.reciprocal(L.denom[:], L.denom[:]))
            for t in range(NT):
                o = (L.M, L.R[0])[t][:, 0:H * w].rearrange("p (h r) -> p h r", r=w)
                i = dve.tensor_tensor(L.AO[:, t, :].rearrange("p (h d) -> p h d", d=DH), o[:, :, 0:DH],
                                      L.denom[:, t, :, None].to_broadcast([P, H, DH]), ALU.mult)
            if U.kind == "ffn":
                i.then_inc(L.ao_ready.sem, 1)
            else:
                link(L, dve, i)
            yield

        def idle(L, eng):
            yield

        def idle_norm(L, eng, n):
            yield
            yield

        def idle_project(L, eng, U):
            for _ in range(4):
                yield


        def pe_project(L, pe, U):
            pe.wait_ge(L.ao_ready.sem, L.ao_ready.at(1))
            for t in range(NT):
                i = pe.transpose(L.M[:, t * P:(t + 1) * P], L.AO[:, t, :], ident[:])
            i.then_inc(L.aoT_ready.sem, 1)
            yield
            yield
            pe.wait_ge(L.aoT_taken.sem, L.aoT_taken.at(1))
            for t in range(NT):
                cols = slice(t * C, (t + 1) * C)
                pe.matmul(L.OB[:, cols], L.aoT[:, t * P:(t + 1) * P], U.wo[:], start=True, stop=False)
                i = pe.matmul(L.OB[:, cols], ones2[:], U.bo2[:], start=False, stop=True)
            i.then_inc(L.y_ready.sem, 1)
            yield
            yield

        def act_project(L, act, U):
            yield
            act.wait_ge(L.aoT_ready.sem, L.aoT_ready.at(1))
            act.copy(L.aoT[:], L.M[:, 0:T]).then_inc(L.aoT_taken.sem, 1)
            yield
            yield
            yield

        def dve_project(L, dve, U):
            yield
            yield
            yield
            dve.wait_ge(L.y_ready.sem, L.y_ready.at(1))
            dve.tensor_tensor(L.res[:], L.resid[:], L.OB[:, 0:NT * C].rearrange("p (t c) -> p t c", t=NT),
                              ALU.add).then_inc(L.res_ready.sem, 1)
            yield


        def run(eng, stages, per=None, last_apart=False):
            even, odd = lanes

            def stage(L, n, p, last=False):
                L.p, L.last = p, last
                if n == 0:
                    L.dve_steps = 0
                return stages[n](L, eng)

            def turn(p, first=False, last=False):
                for n in range(len(stages)):
                    late = (n or len(stages)) - 1
                    if first and n == 0:
                        together([stage(even, n, p)])
                    else:
                        both = [stage(even, n, p, last), stage(odd, late, p if n else p - 1, last and n > 0)]
                        together(both if n % 2 else both[::-1])

            turn(0, first=True)
            with eng.Fori(1, PASSES - int(last_apart)) as p:
                turn(p)
            if last_apart:
                turn(PASSES - 1, last=True)
            even.p = PASSES - 1
            together([stage(odd, len(stages) - 1, PASSES - 1, last_apart)])
            for L in lanes:
                if per is not None and L.dve_steps != per["dve_step"]:
                    raise ValueError(f"dve_step makes {L.dve_steps} in a pass, not {per['dve_step']}")

        def together(live):
            while live:
                for g in list(live):
                    try:
                        next(g)
                    except StopIteration:
                        live.remove(g)

        minus_half = const("minus_half", [P, NT])
        ident_bf = const("ident_bf", [P, P], BF16)
        ident_r = const("ident_r", [P, P], F32R)
        hide = const("hide", [P, P], BF16)
        max_rows = const("max_rows", [P, 1 + S4])
        own_rows = const("own_rows", [P, S4])
        spread = const("spread", [P, S4, len(SPREAD) * 32], F32R)
        for L in lanes:
            L.Q = L.sb("queries", [P, S4, T], F32R)
            L.K = L.sb("keys", [P, H, T], F32R)
            L.V = L.sb("v", [P, NT, H, 32])
            L.probs = L.sb("probs", [P, N_SELF, 512])
            L.HI = L.sb("hi", [P, 2 * T], F32R)
            L.LO = L.sb("lo", [P, 2 * T], F32R)
            L.negmax = L.sb("negmax", [P, NT, S4, S4])
            L.maxparts = L.sb("maxparts", [P, NT, S4, MREND], F32R)
            L.O = L.sb("o", [P, 2, 512])
            L.QK = L.O[:].rearrange("p n q -> p (n q)")[:, 0:2 * T]
            L.AO = L.sb("ao", [P, NT, C])
            L.srcT = L.sb("srcT", [P, T])
            L.aoT = L.srcT
            L.denom = L.sb("denom", [P, NT, H])
            L.KX = L.sb("ctx_keys", [P, S4, S4, TC], F32R)
            L.VX = L.sb("ctx_v", [P, H // 2, 32])
            L.ctxT = L.sb("ctxT", [CC, 2 * TC])
            L.tok = L.sb("tok", [P, NT, C])
            L.x = L.sb("x", [P, NT, C])
            L.res = L.sb("res", [P, NT, C])
            L.x1 = L.sb("x1", [P, NT, C])
            L.x2 = L.sb("x2", [P, NT, C])
            L.resid = L.x2
            L.stats = L.sb("stats", [P, NT, 6])
            L.meanvar = L.sb("meanvar", [P, NT, 2])
            L.vareps = L.sb("vareps", [P, NT])
            L.rstd = L.sb("rstd", [P, NT])
            L.keep2 = L.sb("keep2", [P, NT, 2])
            L.keeprows = L.sb("keeprows", [2, T], F32R)
            L.keep = L.sb("keep", [P, NT])
            L.gone = L.sb("gone", [P, NT])
            L.keybias = L.sb("keybias", [P, NT])
            L.sums = L.sb("sums", [P, NT])
            L.pad8 = L.sb("pad8", [P, NT], U8)
            L.pad = L.sb("pad", [P, NT])
            L.hT = L.srcT
            flat = L.probs[:].rearrange("p r n -> p (r n)")
            L.g = flat[:, 0:2 * FF // P * T].rearrange("p (e c t) -> p e c t", e=2, c=FC)
            flat = flat[:, 2 * FF // P * T:]
            L.w1 = flat[:, 0:K2 * FF].rearrange("p (e f) -> p e f", e=K2)
            L.w2 = flat[:, K2 * FF:2 * K2 * FF].rearrange("p (e c n) -> p e c n", e=K2, c=FC)
            flat = flat[:, 2 * K2 * FF:]
            L.b1 = flat[:, 0:K2 * FC].rearrange("p (e c) -> p e c", e=K2)
            L.b2 = flat[:, K2 * FC:K2 * FC + K2 * C].rearrange("p (e n) -> p e n", e=K2)
            L.y = L.x1
            L.sum = L.AO
            L.logits = L.sb("logits", [P, NT, E])
            L.top = L.sb("top", [P, NT, E])
            L.index = L.sb("index", [P, NT, E], U32)
            L.indexf = L.sb("indexf", [P, NT, E])
            L.diff = L.sb("diff", [P, NT])
            L.tanh = L.sb("tanh", [P, NT])
            L.gate2 = L.sb("gate2", [P, NT, K2])
            L.picked = L.sb("picked", [P, NT, K2, E])
            L.cw = L.sb("cw", [P, NT, E])
            L.hsum = L.sb("hsum", [P, 1])

        w, early, late = {}, [], []
        for n in ("a_wq", "a_wk", "a_wv", "x_wq", "l0_wq", "l0_wk", "l0_wv", "l0_wo"):
            w[n] = const(n, [P, C])
        for n in ("x_wk", "x_wv"):
            w[n] = const(n, [CC, C])
        for n in ("a_bq", "l0_bq", "l0_bk", "l0_ln1_w", "l0_ln1_b"):
            w[n] = const(n, [P, 1])
        for n in ("a_gamma", "a_beta"):
            w[n] = const(n, [P, C])
        for n in w:
            early.append((w[n][:], ins[n].to_broadcast([P, C]) if n in ("a_gamma", "a_beta") else ins[n]))
        row_parts = const("row_parts", [2, ins["rows"].shape[1]], F32R)
        loaded_rows, low_rows = (lanes[n].probs[0:1].rearrange("p r n -> p (r n)")[:, 0:ins["rows"].shape[1]]
                                 for n in range(2))
        low_rows = low_rows.bitcast(F32R)
        early.append((loaded_rows, ins["rows"]))
        place = 0
        for n, width in BIAS_ROWS:
            w[n + "_parts"] = row_parts[:, place:place + width]
            place += width
        w["m0_w1"] = const("m0_w1", [P, E, FF])
        w["m0_w2"] = const("m0_w2", [P, E, FC, C])
        w["m0_b1"] = const("m0_b1", [P, E, FC])
        w["m0_gw"] = const("m0_gw", [P, E])
        w["m0_gb"] = const("m0_gb", [P, E])
        late += [(w["m0_w1"][:, e, :], ins["m0_w1"][e]) for e in range(E)]
        late += [(w["m0_w2"][:, e], ins["m0_w2"][e]) for e in range(E)]
        late += [(w["m0_b1"][:], ins["m0_b1"]), (w["m0_gw"][:], ins["m0_gw"]),
                 (w["m0_gb"][:], ins["m0_gb"].to_broadcast([P, E]))]
        for n in ("l1_wq", "l1_wk", "l1_wv", "l1_wo"):
            w[n] = const(n, [P, C])
        for n in ("m0_lnw", "m0_lnb", "l1_bq", "l1_bk", "l1_ln1_w", "l1_ln1_b", "m1_lnw", "m1_lnb"):
            w[n] = const(n, [P, 1])
        w["m1_gw"] = const("m1_gw", [P, E])
        w["m1_gb"] = const("m1_gb", [1, E])
        late += [(w[n][:], ins[n]) for n in list(w) if n[:2] in ("l1", "m1") and n[-6:] != "_parts" or n[:5] == "m0_ln"]
        number = const("number", [P, E])
        ones_row = const("ones_row", [1, P])

        def load_sequence(L, sp, p):
            lane = lanes.index(L)
            sp.dma_start(L.x[:], token_major(ins["x"], lane, p)).then_inc(L.loaded.sem, 16)
            ctx_src = ins["ctxT"].rearrange("(p l) c k -> l p c k", l=2)[lane][bass.ds(p, 1)].rearrange(
                "o c k -> c (o k)")
            for k in range(2):
                sp.dma_start(L.ctxT[:, k * TC:(k + 1) * TC], ctx_src).then_inc(L.loaded.sem, 16)
            pad_src = ins["pad"].rearrange("(p l) t n -> l p t n", l=2)[lane][bass.ds(p, 1)].rearrange(
                "o t n -> t (o n)")
            sp.dma_start(L.pad8[:], pad_src).then_inc(L.loaded.sem, 16)

        def ones_against_maxima(L, dve):
            for a in range(S4):
                i = dve.tensor_scalar(L.K[MROW:MREND, a::S4, :],
                                      max_rows[MROW:MREND, 0:1, None].to_broadcast([MREND - MROW, S4, T]),
                                      max_rows[MROW:MREND, 1 + a:2 + a], None, ALU.mult)
            return i

        setup_ctx = ExitStack()
        with setup_ctx, nc.Block() as block:
            spread_image = setup_ctx.enter_context(nc.sbuf_tensor("spread_image", [P, S4, len(SPREAD), 32], F32))
            max_row_part = setup_ctx.enter_context(nc.sbuf_tensor("max_row_part", [P, S4, 2], F32))
            row_in_part = setup_ctx.enter_context(nc.sbuf_tensor("row_in_part", [P, S4, 3], F32))

            @block.sync
            def _(sp):
                for dst, src in early:
                    sp.dma_start(dst, src).then_inc(sem_setup_dma, 16)
                for L in lanes:
                    load_sequence(L, sp, 0)

            @block.gpsimd
            def _(pool):
                pool.memset(hide[:], 0.0)
                pool.memset(minus_half[:], -0.5)
                pool.memset(spread_image[:], 0.0)
                pool.memset(row_in_part[:], 1.0)
                pool.memset(max_row_part[:], 0.0)
                pool.memset(ident[:], 0.0).then_inc(sem_setup_pool, 1)
                pool.wait_ge(sem_setup_pool, 1)
                pool.affine_select(out=ident[:], in_=ident[:], compare_op=ALU.not_equal, fill=1.0, base=0,
                                   pattern=[[-1, P]], channel_multiplier=1).then_inc(sem_setup_pool, 1)
                pool.affine_select(out=hide[:], in_=hide[:], compare_op=ALU.is_ge, fill=HIDE, base=0,
                                   pattern=[[-1, P]], channel_multiplier=1).then_inc(sem_setup_pool, 1)
                for s in range(S4):
                    for n, block_used in enumerate(SPREAD):
                        if block_used:
                            i = pool.affine_select(out=spread_image[:, s, n], in_=spread_image[:, s, n],
                                                   compare_op=ALU.not_equal, fill=1.0, base=-s, pattern=[[-S4, 32]],
                                                   channel_multiplier=1)
                pool.affine_select(out=max_row_part[:], in_=max_row_part[:], compare_op=ALU.not_equal, fill=1.0,
                                   base=-MROW, pattern=[[-1, S4], [-S4, 2]],
                                   channel_multiplier=1).then_inc(sem_setup_pool, 1)
                pool.affine_select(out=row_in_part[:], in_=row_in_part[:], compare_op=ALU.is_ge, fill=0.0, base=0,
                                   pattern=[[-8, S4], [-32, 3]], channel_multiplier=1).then_inc(sem_setup_pool, 1)
                pool.wait_ge(sem_setup_pool, 5)
                pool.affine_select(out=row_in_part[:], in_=row_in_part[:], compare_op=ALU.is_ge, fill=0.0, base=7,
                                   pattern=[[8, S4], [32, 3]], channel_multiplier=-1).then_inc(sem_setup_pool, 1)

            @block.vector
            def _(dve):
                dve.wait_ge(sem_setup_pool, 6)
                dve.tensor_copy(ident_bf[:], ident[:])
                dve.tensor_copy(ident_r[:], ident[:])
                dve.tensor_copy(spread[:].rearrange("p s n -> p (s n)"),
                                spread_image[:].rearrange("p s n j -> p (s n j)"))
                dve.memset(max_rows[:, 0:1], 1.0)
                dve.tensor_reduce(max_rows[:, 1:1 + S4], max_row_part[:], AX.X, ALU.add)
                dve.tensor_reduce(own_rows[:], row_in_part[:], AX.X, ALU.add).then_inc(sem_setup, 1)
                dve.memset(ones2[:].bitcast(F32), 1.0).then_inc(sem_setup, 1)
                dve.wait_ge(sem_setup, 2)
                for L in lanes:
                    dve.sem_inc(L.res_stored.sem, 16)
                    dve.sem_inc(L.x2_stored.sem, 16)
        for L in lanes:
            L.res_stored.base = L.x2_stored.base = 16

        with nc.Block() as block:
            @block.sync
            def _(sp):
                sp.wait_ge(sem_setup, 4)
                sp.dma_start(row_parts[1:2, :].bitcast(F32), low_rows.bitcast(F32)).then_inc(sem_setup_dma, 16)
                sp.wait_ge(sem_setup_dma, 16 * (len(early) + 1))

            @block.vector
            def _(dve):
                for L in lanes:
                    ones_against_maxima(L, dve)
                    for a in range(S4):
                        dve.tensor_scalar(L.KX[MROW:MREND, :, a, :],
                                          max_rows[MROW:MREND, 0:1, None].to_broadcast([MREND - MROW, S4, TC]),
                                          max_rows[MROW:MREND, 1 + a:2 + a], None, ALU.mult)
                dve.wait_ge(sem_setup_pool, 7)
                for L in lanes:
                    dve.memset(L.V[:, :, :, DH:DH + 1], 1.0)
                    for k in range(2):
                        dve.memset(L.VX[k * TC:(k + 1) * TC, :, 16 * k + DH:16 * k + DH + 1], 1.0)
                dve.wait_ge(sem_setup_dma, 16 * len(early))
                dve.tensor_copy(row_parts[0:1, :], loaded_rows).then_inc(sem_setup, 1)
                dve.wait_ge(sem_setup, 3)
                dve.tensor_tensor(low_rows, loaded_rows, row_parts[0:1, :].bitcast(F32),
                                  ALU.subtract).then_inc(sem_setup, 1)
                dve.wait_ge(sem_setup, 4)

            @block.gpsimd
            def _(pool):
                for L in lanes:
                    pool.memset(L.V[:], 0.0)
                    i = pool.memset(L.VX[:], 0.0)
                i.then_inc(sem_setup_pool, 1)
                for L in lanes:
                    pool.memset(L.maxparts[:].bitcast(F32), 0.0)
                pool.memset(ones_row[:], 1.0)
                pool.iota(number[:], pattern=[[1, E]], base=0, channel_multiplier=0,
                          allow_small_or_imprecise_dtypes=True).then_inc(sem_setup_pool, 1)
                pool.wait_ge(sem_setup_pool, 8)

        attention_per_unit = dict(tok_ready=1, transposed=1, src_ready=1, projected=2, qk_taken=1, v_taken=1,
                                  split_ready=1, spread_ready=4, stack_by_act=2, stack_by_dve=2, maxparts_ready=1,
                                  maxT_ready=2, maxrows_by_act=1, maxrows_by_dve=1, oT_ready=1)
        project_per = dict(ao_ready=1, aoT_ready=1, aoT_taken=1, y_ready=1, res_ready=1, res_stored=16)

        def first_attentions():
            A = Unit("self", 0, 0, 0, 0, wq=w["a_wq"], wk=w["a_wk"], wv=w["a_wv"], bq=w["a_bq"], bk2=w["a_bk_parts"],
                     bv2=w["a_bv_parts"])
            X = Unit("ctx", 1, N_SELF, 2, N_SELF, wq=w["x_wq"], wk=w["x_wk"], wv=w["x_wv"])
            F0 = Unit("ffn", 2, N_SELF + N_CTX, 3, N_SELF, wq=w["l0_wq"], wk=w["l0_wk"], wv=w["l0_wv"], wo=w["l0_wo"],
                      bq=w["l0_bq"], bk=w["l0_bk"], bv2=w["l0_bv_parts"], bo2=w["l0_bo_parts"], ln_w=w["l0_ln1_w"],
                      ln_b=w["l0_ln1_b"])
            per = {k: 3 * v for k, v in attention_per_unit.items()} | project_per
            rounds = 2 * N_SELF + N_CTX
            per |= dict(scores_ready=rounds, max_taken=rounds, st_ready=rounds, exp_done=rounds, masked=2 * N_SELF,
                        pv_done=5, o_taken=5, loaded=64, x2_ready=1, x2_stored=16, ln_var=4, ln_rstd=4,
                        dve_step=28)
            for L in lanes:
                L.begin_phase(per)

            def dve_a_scores(L, dve):
                dve.wait_ge(L.loaded.sem, L.loaded.at(64))
                dve.tensor_copy(L.pad[:], L.pad8[:])
                link(L, dve, dve.tensor_reduce(L.sums[:], L.x[:], AX.X, ALU.add))
                link(L, dve, dve.tensor_scalar(L.gone[:], L.sums[:], 0.0, None, ALU.is_equal))
                dve.tensor_scalar(L.keybias[:], L.gone[:], -BIG, None, ALU.mult)
                dve.tensor_scalar(L.keep2[:], L.gone[:, :, None].to_broadcast([P, NT, 2]), -1.0, 1.0, ALU.mult, ALU.add)
                link(L, dve, dve.tensor_scalar(L.keep[:], L.gone[:], -1.0, 1.0, ALU.mult, ALU.add))
                for t in range(NT):
                    i = dve.tensor_scalar(L.tok[:, t, :], L.x[:, t, :], L.keep[:, t:t + 1], None, ALU.mult)
                i.then_inc(L.tok_ready.sem, 1)
                dve.wait_ge(L.x2_stored.sem, L.x2_stored.at(0))
                dve.tensor_tensor(L.x2[:], L.x[:], w["a_beta"][:, None, :].to_broadcast([P, NT, C]), ALU.add)
                yield from dve_scores(L, dve, A)

            def dve_a_values(L, dve):
                yield from dve_values(L, dve, A)
                dve.wait_ge(L.res_stored.sem, L.res_stored.at(0))
                for t in range(NT):
                    i = dve.scalar_tensor_tensor(L.res[:, t, :], L.AO[:, t, :], L.keep[:, t:t + 1], L.x[:, t, :],
                                                 ALU.mult, ALU.add)
                link(L, dve, i)
                yield from dve_layer_norm(L, dve, L.res, 0, L.AO, w["a_gamma"], L.x2, eps=1e-8)
                yield from dve_layer_norm(L, dve, L.AO, 1, L.x1)
                for t in range(NT):
                    i = dve.tensor_scalar(L.tok[:, t, :], L.x1[:, t, :], L.pad[:, t:t + 1], None, ALU.mult)
                i.then_inc(L.tok_ready.sem, 1)
                yield

            def dve_x_scores(L, dve):
                yield from dve_scores(L, dve, X)

            def dve_x_values(L, dve):
                yield from dve_values(L, dve, X)
                link(L, dve, dve.tensor_tensor(L.res[:], L.AO[:], L.x1[:], ALU.add))
                yield from dve_layer_norm(L, dve, L.res, 2, L.x2, ready=L.x2_ready)
                dve.wait_ge(L.x2_ready.sem, L.x2_ready.at(1))
                yield from dve_layer_norm(L, dve, L.x2, 3, L.tok, ready=L.tok_ready)
                yield

            def dve_f_scores(L, dve):
                yield from dve_scores(L, dve, F0)

            def dve_f_values(L, dve):
                yield from dve_values(L, dve, F0)
                yield from dve_project(L, dve, F0)

            def attention_stages(scores, values, norm, project):
                def of(*parts):
                    def stage(L, eng):
                        for part, which in parts:
                            yield from part(L, eng, which)
                    return stage
                return [of((scores, A)), of((values, A), (norm, 0), (norm, 1)),
                        of((scores, X)), of((values, X), (norm, 2), (norm, 3)),
                        of((scores, F0)), of((values, F0), (project, F0))]

            def sp_store_x2(L, sp):
                if not L.last:
                    sp.wait_ge(L.tok_ready.sem, L.tok_ready.at(2))
                    sp.sem_inc(held_sp, 1)
                    sp.wait_ge(L.projected.sem, L.projected.at(4))
                    sp.sem_inc(held_sp, 1)
                    load_sequence(L, sp, L.p + 1)
                sp.wait_ge(L.x2_ready.sem, L.x2_ready.at(1))
                sp.sem_inc(held_sp, 1)
                sp.dma_start(scratch(scratch_x2, lanes.index(L), L.p), L.x2[:]).then_inc(L.x2_stored.sem, 16)
                yield

            def sp_store(L, sp):
                for _ in range(3):
                    yield
                sp.wait_ge(L.res_ready.sem, L.res_ready.at(1))
                sp.sem_inc(held_sp, 1)
                sp.dma_start(scratch(scratch_a, lanes.index(L), L.p), L.res[:]).then_inc(L.res_stored.sem, 16)
                yield

            with nc.Block() as block:
                @block.sync
                def _(sp):
                    for dst, src in late:
                        sp.dma_start(dst, src).then_inc(sem_late_dma, 16)
                    run(sp, [idle, idle, idle, sp_store_x2, idle, sp_store], last_apart=True)
                    for L in lanes:
                        sp.wait_ge(L.res_stored.sem, L.res_stored.at(16))
                        sp.wait_ge(L.x2_stored.sem, L.x2_stored.at(16))
                    sp.wait_ge(sem_late_dma, 16 * len(late))

                @block.tensor
                def _(pe):
                    run(pe, attention_stages(pe_scores, pe_values, idle_norm, pe_project))

                @block.scalar
                def _(act):
                    run(act, attention_stages(act_scores, act_values, idle_norm, act_project))

                @block.vector
                def _(dve):
                    run(dve, [dve_a_scores, dve_a_values, dve_x_scores, dve_x_values, dve_f_scores, dve_f_values], per)

                @block.gpsimd
                def _(pool):
                    run(pool, attention_stages(pool_scores, pool_values, pool_layer_norm, idle_project))

        moe_per = dict(loaded=16, tok_ready=1, transposed=1, src_ready=1, res_ready=1, res_stored=16, gate_ready=1)

        def pe_experts(L, pe, n, w1_hi, w1_lo, w2, b2rows):
            hT_hi, hT_lo = L.HI[:, 0:T], L.LO[:, 0:T]
            pe.wait_ge(L.split_ready.sem, L.split_ready.at(1))
            def outputs(e):
                pe.wait_ge(L.gelu_done.sem, L.gelu_done.at(2 * (e + 1)))
                if e >= 2:
                    pe.wait_ge(L.acc_done.sem, L.acc_done.at(e - 1))
                y = (L.OB, L.M)[e % 2]
                for t in range(NT):
                    for c in range(FC):
                        i = pe.matmul(y[:, t * C:(t + 1) * C], L.g[:, e % 2, c, t * P:(t + 1) * P], w2(e, c),
                                      start=(c == 0), stop=False)
                    i = pe.matmul(y[:, t * C:(t + 1) * C], ones2[:], b2rows(e), start=False, stop=True)
                i.then_inc(L.expert_y.sem, 1)

            for e in range(n):
                for half in range(2):
                    if e >= 1:
                        pe.wait_ge(L.gelu_done.sem, L.gelu_done.at(2 * e - 1 + half))
                    for k in range(2):
                        to, c = L.R[half][:, k * T:(k + 1) * T], 2 * half + k
                        pe.matmul(to, w1_hi(e, c), hT_hi, start=True, stop=False)
                        pe.matmul(to, w1_hi(e, c), hT_lo, start=False, stop=False)
                        i = pe.matmul(to, w1_lo(e, c), hT_hi, start=False, stop=True)
                    i.then_inc(L.hidden_ready.sem, 1)
                if e >= 1:
                    outputs(e - 1)
                yield
            outputs(n - 1)
            yield

        def act_experts(L, act, n, b1):
            for e in range(n):
                if e >= 2:
                    act.wait_ge(L.expert_y.sem, L.expert_y.at(e - 1))
                for half in range(2):
                    act.wait_ge(L.hidden_ready.sem, L.hidden_ready.at(2 * e + half + 1))
                    for k in range(2):
                        c = 2 * half + k
                        i = act.activation(L.g[:, e % 2, c, :], L.R[half][:, k * T:(k + 1) * T], ACT.Gelu,
                                           bias=b1(e, c))
                    i.then_inc(L.gelu_done.sem, 1)
                yield
            yield

        first_attentions()

        def token_experts():
            w1, w2, b1, b2rows = (w[n] for n in ("m0_w1", "m0_w2", "m0_b1", "m0_b2_parts"))
            gw, gb, lnw, lnb = (w[n] for n in ("m0_gw", "m0_gb", "m0_lnw", "m0_lnb"))
            w1_hi, w1_lo = (L.K[:].rearrange("p h k -> p (h k)").rearrange("p (e f) -> p e f", e=E) for L in lanes)
            with nc.Block() as block:
                @block.scalar
                def _(act):
                    for e in range(E):
                        act.copy(w1_hi[:, e], w1[:, e]).then_inc(sem_w1_hi, 1)

                @block.vector
                def _(dve):
                    for e in range(E):
                        dve.wait_ge(sem_w1_hi, e + 1)
                        i = dve.tensor_tensor(w1_lo[:, e], w1[:, e], w1_hi[:, e].bitcast(F32), ALU.subtract)
                    i.then_inc(sem_setup, 1)
                    dve.wait_ge(sem_setup, 5)

            per = moe_per | dict(split_ready=1, ln_var=1, ln_rstd=1, gate_diff=1, gate_w=1, hidden_ready=2 * E,
                                 gelu_done=2 * E, expert_y=E, acc_done=E, dve_step=10)
            for L in lanes:
                L.begin_phase(per)

            def dve_gate(L, dve):
                yield
                yield
                dve.wait_ge(L.loaded.sem, L.loaded.at(16))
                yield from dve_layer_norm(L, dve, L.x, 0, L.tok, ready=L.tok_ready)
                yield
                yield
                dve.wait_ge(L.src_ready.sem, L.src_ready.at(1))
                link(L, dve, dve.tensor_copy(L.HI[:, 0:T], L.hT[:]))
                dve.tensor_tensor(L.LO[:, 0:T], L.hT[:], L.HI[:, 0:T].bitcast(F32),
                                  ALU.subtract).then_inc(L.split_ready.sem, 1)
                yield
                dve.wait_ge(L.gate_ready.sem, L.gate_ready.at(1))
                link(L, dve, dve.tensor_tensor(L.logits[:], L.OB[:, 0:NT * E].rearrange("p (t e) -> p t e", t=NT),
                                               gb[:, None, :].to_broadcast([P, NT, E]), ALU.add), apart=True)
                for t in range(NT):
                    i = dve.max(L.top[:, t, :], L.logits[:, t, :])
                link(L, dve, i)
                dve.tensor_tensor(L.diff[:], L.top[:, :, 0], L.top[:, :, 1], ALU.subtract).then_inc(L.gate_diff.sem, 1)
                for t in range(NT):
                    i = dve.max_index(L.index[:, t, :], L.top[:, t, :], L.logits[:, t, :])
                link(L, dve, i)
                link(L, dve, dve.tensor_copy(L.indexf[:], L.index[:]))
                yield
                yield
                dve.wait_ge(L.gate_w.sem, L.gate_w.at(1))
                dve.tensor_scalar(L.gate2[:, :, 0], L.tanh[:], 0.5, 0.5, ALU.mult, ALU.add)
                link(L, dve, dve.tensor_scalar(L.gate2[:, :, 1], L.tanh[:], -0.5, 0.5, ALU.mult, ALU.add))
                for t in range(NT):
                    for k in range(K2):
                        i = dve.tensor_scalar(L.picked[:, t, k, :], number[:], L.indexf[:, t, k:k + 1],
                                              L.gate2[:, t, k:k + 1], ALU.is_equal, ALU.mult)
                link(L, dve, i)
                link(L, dve, dve.tensor_tensor(L.cw[:], L.picked[:, :, 0, :], L.picked[:, :, 1, :], ALU.add))
                yield

            def weigh(L, dve, e):
                yield
                dve.wait_ge(L.expert_y.sem, L.expert_y.at(e + 1))
                y = (L.OB, L.M)[e % 2]
                before = L.x if e == 0 else L.res
                for t in range(NT):
                    i = dve.scalar_tensor_tensor(L.res[:, t, :], y[:, t * C:(t + 1) * C], L.cw[:, t, e:e + 1],
                                                 before[:, t, :], ALU.mult, ALU.add)
                i.then_inc(L.acc_done.sem, 1)
                dve.wait_ge(L.acc_done.sem, L.acc_done.at(e + 1))

            def dve_experts(L, dve):
                dve.wait_ge(L.res_stored.sem, L.res_stored.at(0))
                for e in range(E):
                    yield from weigh(L, dve, e)
                dve.tensor_copy(L.diff[:], L.tanh[:]).then_inc(L.res_ready.sem, 1)
                yield

            def pe_gate(L, pe):
                for _ in range(4):
                    yield
                pe.wait_ge(L.tok_ready.sem, L.tok_ready.at(1))
                for t in range(NT):
                    i = pe.transpose(L.M[:, t * P:(t + 1) * P], L.tok[:, t, :], ident[:])
                i.then_inc(L.transposed.sem, 1)
                yield
                yield
                pe.wait_ge(L.src_ready.sem, L.src_ready.at(1))
                for t in range(NT):
                    i = pe.matmul(L.OB[:, t * E:(t + 1) * E], L.hT[:, t * P:(t + 1) * P], gw[:], start=True, stop=True)
                i.then_inc(L.gate_ready.sem, 1)
                yield
                yield
                yield

            def act_gate(L, act):
                for _ in range(5):
                    yield
                act.wait_ge(L.transposed.sem, L.transposed.at(1))
                act.activation(L.hT[:], L.M[:, 0:T], ACT.Identity, bias=lnb[:], scale=lnw[:]).then_inc(L.src_ready.sem, 1)
                yield
                yield
                yield
                act.wait_ge(L.gate_diff.sem, L.gate_diff.at(1))
                act.activation(L.tanh[:], L.diff[:], ACT.Tanh, scale=0.5).then_inc(L.gate_w.sem, 1)
                yield

            def pe_token_experts(L, pe):
                yield from pe_experts(L, pe, E, lambda e, c: w1_hi[:, e, c * P:(c + 1) * P],
                                      lambda e, c: w1_lo[:, e, c * P:(c + 1) * P], lambda e, c: w2[:, e, c, :],
                                      lambda e: b2rows[:, e * C:(e + 1) * C])

            def act_token_experts(L, act):
                yield from act_experts(L, act, E, lambda e, c: b1[:, e, c:c + 1])

            def sp_load(L, sp, p):
                sp.dma_start(L.x[:], scratch(scratch_a, lanes.index(L), p)).then_inc(L.loaded.sem, 16)

            def sp_store(L, sp):
                if not L.last:
                    sp.wait_ge(L.acc_done.sem, L.acc_done.at(1))
                    sp.sem_inc(held_sp, 1)
                    sp_load(L, sp, L.p + 1)
                for _ in range(3):
                    yield
                sp.wait_ge(L.res_ready.sem, L.res_ready.at(1))
                sp.sem_inc(held_sp, 1)
                sp.dma_start(scratch(scratch_b, lanes.index(L), L.p), L.res[:]).then_inc(L.res_stored.sem, 16)
                yield

            def pool_gate(L, pool):
                yield
                yield
                yield from pool_layer_norm(L, pool, 0)

            with nc.Block() as block:
                @block.sync
                def _(sp):
                    for L in lanes:
                        sp_load(L, sp, 0)
                    run(sp, [idle, sp_store], last_apart=True)
                    for L in lanes:
                        sp.wait_ge(L.res_stored.sem, L.res_stored.at(16))

                @block.tensor
                def _(pe):
                    run(pe, [pe_gate, pe_token_experts])

                @block.scalar
                def _(act):
                    run(act, [act_gate, act_token_experts])

                @block.vector
                def _(dve):
                    run(dve, [dve_gate, dve_experts], per)

                @block.gpsimd
                def _(pool):
                    run(pool, [pool_gate, idle])

        token_experts()

        def second_attention():
            F1 = Unit("ffn", 0, 0, 0, 0, wq=w["l1_wq"], wk=w["l1_wk"], wv=w["l1_wv"], wo=w["l1_wo"],
                      bq=w["l1_bq"], bk=w["l1_bk"], bv2=w["l1_bv_parts"], bo2=w["l1_bo_parts"], ln_w=w["l1_ln1_w"],
                      ln_b=w["l1_ln1_b"])
            with nc.Block() as block:
                @block.vector
                def _(dve):
                    for L in lanes:
                        i = ones_against_maxima(L, dve)
                    i.then_inc(sem_setup, 1)
                    dve.wait_ge(sem_setup, 6)

            per = attention_per_unit | project_per
            per |= dict(scores_ready=N_SELF, max_taken=N_SELF, st_ready=N_SELF, exp_done=N_SELF, masked=N_SELF,
                        pv_done=2, o_taken=2, loaded=16, resid_ready=1, ln_var=1, ln_rstd=1, dve_step=5)
            for L in lanes:
                L.begin_phase(per)

            def dve_first(L, dve):
                dve.wait_ge(L.loaded.sem, L.loaded.at(16))
                yield from dve_layer_norm(L, dve, L.x, 0, L.tok, ready=L.tok_ready)
                yield from dve_scores(L, dve, F1)

            def dve_second(L, dve):
                yield from dve_values(L, dve, F1)
                dve.wait_ge(L.res_stored.sem, L.res_stored.at(0))
                dve.wait_ge(L.resid_ready.sem, L.resid_ready.at(1))
                yield from dve_project(L, dve, F1)

            def keep_residual(L, act):
                act.wait_ge(L.loaded.sem, L.loaded.at(16))
                act.wait_ge(L.res_ready.sem, L.res_ready.at(0))
                act.copy(L.resid[:], L.x[:]).then_inc(L.resid_ready.sem, 1)

            def attention_stages(scores, values, norm, project):
                def first(L, eng):
                    if scores is act_scores:
                        keep_residual(L, eng)
                    yield from norm(L, eng, 0)
                    yield from scores(L, eng, F1)

                def second(L, eng):
                    yield from values(L, eng, F1)
                    yield from project(L, eng, F1)
                return [first, second]

            def sp_load(L, sp, p):
                sp.dma_start(L.x[:], scratch(scratch_b, lanes.index(L), p)).then_inc(L.loaded.sem, 16)

            def sp_store(L, sp):
                if not L.last:
                    sp.wait_ge(L.tok_ready.sem, L.tok_ready.at(1))
                    sp.sem_inc(held_sp, 1)
                    sp.wait_ge(L.resid_ready.sem, L.resid_ready.at(1))
                    sp.sem_inc(held_sp, 1)
                    sp_load(L, sp, L.p + 1)
                for _ in range(3):
                    yield
                sp.wait_ge(L.res_ready.sem, L.res_ready.at(1))
                sp.sem_inc(held_sp, 1)
                sp.dma_start(scratch(scratch_a, lanes.index(L), L.p), L.res[:]).then_inc(L.res_stored.sem, 16)
                yield

            with nc.Block() as block:
                @block.sync
                def _(sp):
                    for L in lanes:
                        sp_load(L, sp, 0)
                    run(sp, [idle, sp_store], last_apart=True)
                    for L in lanes:
                        sp.wait_ge(L.res_stored.sem, L.res_stored.at(16))

                @block.tensor
                def _(pe):
                    run(pe, attention_stages(pe_scores, pe_values, idle_norm, pe_project))

                @block.scalar
                def _(act):
                    run(act, attention_stages(act_scores, act_values, idle_norm, act_project))

                @block.vector
                def _(dve):
                    run(dve, [dve_first, dve_second], per)

                @block.gpsimd
                def _(pool):
                    run(pool, attention_stages(pool_scores, pool_values, pool_layer_norm, idle_project))

        second_attention()

        def sequence_experts():
            gw, gb, lnw, lnb = (w[n] for n in ("m1_gw", "m1_gb", "m1_lnw", "m1_lnb"))
            for L in lanes:
                L.logits, L.top, L.index = L.logits[0:1, 0], L.top[0:1, 0], L.index[0:1, 0]
                L.diff, L.tanh, L.gate2 = L.diff[0:1, 0:1], L.tanh[0:1, 0:1], L.gate2[0:1, 0]
                L.cw = L.cw[:, 0, 0:K2]
            per = moe_per | dict(loaded=32, ln_var=2, ln_rstd=2, gate_diff=1, gate_w=1, gate_row=1,
                                 gate_bcast=1, sums_ready=1, hidden_ready=2 * K2, gelu_done=2 * K2, expert_y=K2,
                                 acc_done=K2, expert_chosen=1, expert_loaded=16 * 4 * K2, dve_step=11)
            for L in lanes:
                L.begin_phase(per)


            def dve_gate(L, dve):
                dve.wait_ge(L.loaded.sem, L.loaded.at(32))
                dve.wait_ge(L.res_ready.sem, L.res_ready.at(0))
                dve.tensor_tensor(L.sum[:], L.x[:], L.x2[:], ALU.add).then_inc(L.sums_ready.sem, 1)
                yield from dve_layer_norm(L, dve, L.x, 0, L.tok, ready=L.tok_ready)
                yield from pause(2, 3)
                dve.wait_ge(L.gate_ready.sem, L.gate_ready.at(1))
                link(L, dve, dve.scalar_tensor_tensor(L.logits, L.OB[0:1, 0:E], 1.0 / T, gb[:], ALU.mult, ALU.add), apart=True)
                link(L, dve, dve.max(L.top, L.logits))
                dve.tensor_tensor(L.diff, L.top[:, 0:1], L.top[:, 1:2], ALU.subtract).then_inc(L.gate_diff.sem, 1)
                dve.max_index(L.index, L.top, L.logits).then_inc(L.expert_chosen.sem, 1)
                yield from pause(3, 5)
                dve.wait_ge(L.gate_w.sem, L.gate_w.at(1))
                dve.tensor_scalar(L.gate2[:, 0:1], L.tanh, 0.5, 0.5, ALU.mult, ALU.add)
                dve.tensor_scalar(L.gate2[:, 1:2], L.tanh, -0.5, 0.5, ALU.mult, ALU.add).then_inc(L.gate_row.sem, 1)
                yield
                dve.wait_ge(L.gate_bcast.sem, L.gate_bcast.at(1))
                link(L, dve, dve.tensor_copy(L.cw, L.OB[:, 0:K2]))
                yield

            def dve_experts(L, dve):
                yield from pause(0, 3)
                for e in range(K2):
                    yield
                    dve.wait_ge(L.expert_y.sem, L.expert_y.at(e + 1))
                    y = (L.M, L.R[1])[e]
                    dve.wait_ge(L.expert_loaded.sem, L.expert_loaded.at(16 * 4 * K2))
                    link(L, dve, dve.tensor_tensor(L.y[:], y[:, 0:NT * C].rearrange("p (t c) -> p t c", t=NT),
                                                   L.b2[:, e, None, :].to_broadcast([P, NT, C]), ALU.add))
                    link(L, dve, dve.scalar_tensor_tensor(L.sum[:].rearrange("p t c -> p (t c)"),
                                                          L.y[:].rearrange("p t c -> p (t c)"), L.cw[:, e:e + 1],
                                                          L.sum[:].rearrange("p t c -> p (t c)"), ALU.mult, ALU.add))
                yield
                dve.wait_ge(L.res_stored.sem, L.res_stored.at(0))
                yield from dve_layer_norm(L, dve, L.sum, 1, L.res, ready=L.res_ready)
                yield

            def pe_gate(L, pe):
                yield from pause(0, 2)
                pe.wait_ge(L.tok_ready.sem, L.tok_ready.at(1))
                for t in range(NT):
                    i = pe.transpose(L.M[:, t * P:(t + 1) * P], L.tok[:, t, :], ident[:])
                i.then_inc(L.transposed.sem, 1)
                yield from pause(2, 3)
                pe.wait_ge(L.src_ready.sem, L.src_ready.at(1))
                pe.matmul(L.OB[0:1, 0:E], L.hsum[:], gw[:], start=True, stop=True).then_inc(L.gate_ready.sem, 1)
                yield from pause(3, 6)
                pe.wait_ge(L.gate_row.sem, L.gate_row.at(1))
                pe.matmul(L.OB[:, 0:K2], ones_row[:], L.gate2, start=True, stop=True).then_inc(L.gate_bcast.sem, 1)
                yield

            def pe_two_experts(L, pe):
                yield
                pe.wait_ge(L.expert_loaded.sem, L.expert_loaded.at(16 * 4 * K2))

                def outputs(e):
                    pe.wait_ge(L.gelu_done.sem, L.gelu_done.at(2 * (e + 1)))
                    y = (L.M, L.R[1])[e]
                    for t in range(NT):
                        for c in range(FC):
                            i = pe.matmul(y[:, t * C:(t + 1) * C], L.g[:, e, c, t * P:(t + 1) * P], L.w2[:, e, c, :],
                                          start=(c == 0), stop=(c == FC - 1))
                    i.then_inc(L.expert_y.sem, 1)

                for e in range(K2):
                    for half in range(2):
                        if e >= 1:
                            pe.wait_ge(L.gelu_done.sem, L.gelu_done.at(2 * e - 1 + half))
                        for k in range(2):
                            c = 2 * half + k
                            i = pe.matmul(L.R[half][:, k * T:(k + 1) * T], L.w1[:, e, c * P:(c + 1) * P], L.hT[:],
                                          start=True, stop=True)
                        i.then_inc(L.hidden_ready.sem, 1)
                    yield from pause(2 * e + 1, 3 + e)
                outputs(0)
                yield
                outputs(1)
                yield

            def act_gate(L, act):
                yield from pause(0, 2)
                act.wait_ge(L.transposed.sem, L.transposed.at(1))
                act.activation(L.hT[:], L.M[:, 0:T], ACT.Identity, bias=lnb[:], scale=lnw[:],
                               accum_out=L.hsum[:]).then_inc(L.src_ready.sem, 1)
                yield from pause(2, 4)
                act.wait_ge(L.gate_diff.sem, L.gate_diff.at(1))
                act.activation(L.tanh, L.diff, ACT.Tanh, scale=0.5).then_inc(L.gate_w.sem, 1)
                yield

            def act_two_experts(L, act):
                yield
                for e in range(K2):
                    for half in range(2):
                        act.wait_ge(L.hidden_ready.sem, L.hidden_ready.at(2 * e + half + 1))
                        for k in range(2):
                            c = 2 * half + k
                            i = act.activation(L.g[:, e, c, :], L.R[half][:, k * T:(k + 1) * T], ACT.Gelu,
                                               bias=L.b1[:, e, c:c + 1])
                        i.then_inc(L.gelu_done.sem, 1)
                    yield
                    yield

            def sp_load(L, sp, p):
                lane = lanes.index(L)
                sp.dma_start(L.x[:], scratch(scratch_a, lane, p)).then_inc(L.loaded.sem, 16)
                sp.dma_start(L.x2[:], scratch(scratch_x2, lane, p)).then_inc(L.loaded.sem, 16)

            def sp_gate(L, sp):
                yield from pause(0, 4)
                sp.wait_ge(L.expert_chosen.sem, L.expert_chosen.at(1))
                sp.sem_inc(held_sp, 1)
                for k in range(K2):
                    e = sp.value_load(L.index[0:1, k:k + 1], min_val=0, max_val=E - 1)
                    one = lambda d, s: d[bass.ds(e, 1)].rearrange(s)
                    sp.dma_start(L.w1[:, k, :], one(ins["m1_w1"], "o p f -> p (o f)")).then_inc(L.expert_loaded.sem, 16)
                    sp.dma_start(L.w2[:, k], one(ins["m1_w2"], "o p c n -> p (o c) n")).then_inc(L.expert_loaded.sem, 16)
                    sp.dma_start(L.b1[:, k], one(ins["m1_b1"], "o p c -> p (o c)")).then_inc(L.expert_loaded.sem, 16)
                    sp.dma_start(L.b2[:, k], ins["m1_b2"][bass.ds(e, 1)].to_broadcast([P, C])).then_inc(
                        L.expert_loaded.sem, 16)
                yield

            def sp_store(L, sp):
                if not L.last:
                    sp.wait_ge(L.tok_ready.sem, L.tok_ready.at(1))
                    sp.sem_inc(held_sp, 1)
                    sp.wait_ge(L.sums_ready.sem, L.sums_ready.at(1))
                    sp.sem_inc(held_sp, 1)
                    sp_load(L, sp, L.p + 1)
                yield from pause(0, 8)
                sp.wait_ge(L.res_ready.sem, L.res_ready.at(1))
                sp.sem_inc(held_sp, 1)
                sp.dma_start(token_major(out, lanes.index(L), L.p), L.res[:]).then_inc(L.res_stored.sem, 16)
                yield

            def pool_gate(L, pool):
                yield from pool_layer_norm(L, pool, 0)

            def pool_last_norm(L, pool):
                yield from pause(0, 6)
                yield from pool_layer_norm(L, pool, 1)

            with nc.Block() as block:
                @block.sync
                def _(sp):
                    for L in lanes:
                        sp_load(L, sp, 0)
                    run(sp, [sp_gate, sp_store], last_apart=True)
                    for L in lanes:
                        sp.wait_ge(L.res_stored.sem, L.res_stored.at(16))

                @block.tensor
                def _(pe):
                    run(pe, [pe_gate, pe_two_experts])

                @block.scalar
                def _(act):
                    run(act, [act_gate, act_two_experts])

                @block.vector
                def _(dve):
                    run(dve, [dve_gate, dve_experts], per)

                @block.gpsimd
                def _(pool):
                    run(pool, [pool_gate, pool_last_norm])


        sequence_experts()



def _by_lane(a):
    return a.reshape(a.shape[:-1] + (S4, S4, DH)).swapaxes(-3, -2).swapaxes(-2, -1).reshape(a.shape)


def _layout(i):
    d = {"x": i["x"], "ctxT": i["ctx_768"].transpose(0, 2, 1),
         "pad": i["mask_BxS_bk0"].reshape(B, NT, P).transpose(0, 2, 1)}
    d["a_wq"], d["a_wk"], d["a_wv"] = _by_lane(i["L0_attn_Wq"]), _by_lane(i["L0_attn_Wk"]), i["L0_attn_Wv"]
    d["a_bq"] = _by_lane(i["L0_attn_bq"]).reshape(C, 1)
    d["a_bk"] = _by_lane(i["L0_attn_bk"]).reshape(1, C)
    d["a_bv"] = i["L0_attn_bv"].reshape(1, C)
    d["a_gamma"] = i["L0_attn_gamma"].reshape(1, C)
    d["a_beta"] = i["L0_attn_beta"].reshape(1, C)
    d["x_wq"] = _by_lane(i["L0_xattn_Wq"].T)
    d["x_wk"] = _by_lane(i["L0_xattn_Wkv"][:C].T)
    d["x_wv"] = i["L0_xattn_Wkv"][C:].T
    for n in range(2):
        f = lambda k: i["L0_ffn_" + k][n]
        d[f"l{n}_wq"], d[f"l{n}_wk"] = _by_lane(f("wq")), _by_lane(f("wk"))
        d[f"l{n}_wv"], d[f"l{n}_wo"] = f("wv"), f("wo")
        d[f"l{n}_bq"], d[f"l{n}_bk"] = _by_lane(f("bq")).reshape(C, 1), _by_lane(f("bk")).reshape(C, 1)
        d[f"l{n}_bv"], d[f"l{n}_bo"] = f("bv").reshape(1, C), f("bo").reshape(1, C)
        d[f"l{n}_ln1_w"], d[f"l{n}_ln1_b"] = f("ln1_w").reshape(C, 1), f("ln1_b").reshape(C, 1)
        d[f"m{n}_lnw"], d[f"m{n}_lnb"] = f("ln2_w").reshape(C, 1), f("ln2_b").reshape(C, 1)
        d[f"m{n}_gw"], d[f"m{n}_gb"] = f("gate_w"), f("gate_b").reshape(1, E)
        d[f"m{n}_w1"] = f("e_w1")
        d[f"m{n}_w2"] = f("e_w2").reshape(E, FC, P, C).transpose(0, 2, 1, 3)
        b1 = f("e_b1").reshape(E, FC, P)
        d[f"m{n}_b1"] = b1.transpose(2, 0, 1) if n == 0 else b1.transpose(0, 2, 1)
        d[f"m{n}_b2"] = f("e_b2").reshape(1, E * C) if n == 0 else f("e_b2")
    d["rows"] = np.concatenate([d[n].reshape(1, width) for n, width in BIAS_ROWS], axis=1)
    for n, _ in BIAS_ROWS:
        del d[n]
    return {k: np.ascontiguousarray(v) for k, v in d.items()}


def kernel(**inputs):
    import concourse.bacc as _bacc
    from concourse.bass_utils import run_bass_kernel_spmd as _run

    arrays = _layout({k: np.asarray(v) for k, v in inputs.items()})
    nc = _bacc.Bacc("TRN2", target_bir_lowering=False, num_devices=1)
    ins = {k: nc.dram_tensor(f"in_{k}", a.shape, mybir.dt.from_np(a.dtype), kind="ExternalInput").ap()
           for k, a in arrays.items()}
    out = nc.dram_tensor("out", (B, T, C), F32, kind="ExternalOutput").ap()
    decoder(nc, ins, out)
    r = _run(nc, [{f"in_{k}": a for k, a in arrays.items()}], core_ids=[0])
    return r.results[0]["out"]
```
